# Optimizing a Trainium2 kernel written in Bass

```python
import numpy as np
import jax
import jax.numpy as jnp

def _softmax(x, axis=-1):
    return jax.nn.softmax(x, axis=axis)

def _gelu(x):
    return jax.nn.gelu(x, approximate=True)

def _silu(x):
    return jax.nn.silu(x)

def _sigmoid(x):
    return jax.nn.sigmoid(x)

def _layernorm(x, axis=-1, eps=1e-05):
    m = jnp.mean(x, axis=axis, keepdims=True)
    v = jnp.var(x, axis=axis, keepdims=True)
    return (x - m) / jnp.sqrt(v + eps)

def _scatter_add(tgt, idx, src, axis=0):
    return tgt.at[idx].add(src)

def _segment_sum(src, seg, n):
    return jax.ops.segment_sum(src, seg, n)
kernel_name = 'mk_adj_resnorm_d2_adj_r2_372e08'

def setup_inputs(seed: int=0):
    np.random.seed(seed)
    _w = jnp.asarray

    def _rec_inputs():
        import jax
        import jax.numpy as jnp
        _gk = jax.random.key(seed)
        x = -0.0004776 + 1.001 * jax.random.normal(jax.random.fold_in(_gk, 1), (1354, 512), jnp.float32)
        _a = jax.random.bernoulli(jax.random.fold_in(_gk, 2), 0.0118168, (1354, 1354))
        _a = jnp.logical_or(_a, jnp.eye(1354, dtype=bool))
        _af = _a.astype(jnp.float32)
        adj = _af
        return (x, adj)
    x, adj = _rec_inputs()

    def _L0_gnn_setup():
        import jax, jax.numpy as jnp
        import numpy as np
        N, H, E, HEADS = (1500, 512, 10000, 8)
        DK = H // HEADS
        key = jax.random.key(seed)
        k1, k2, k3, k4 = jax.random.split(key, 4)
        inst_feature = jax.random.normal(k1, (N, H), dtype=jnp.float32)
        rel_pair_index = jax.random.randint(k2, (E, 2), 0, N, dtype=jnp.int64)
        agg = jnp.zeros((N, N), dtype=jnp.float32)
        agg = agg.at[rel_pair_index[:, 0], rel_pair_index[:, 1]].set(1.0)
        agg = agg.at[jnp.arange(N), jnp.arange(N)].set(1.0)
        std = float(np.sqrt(2.0 / (H + DK)))
        Wq = jax.random.normal(k3, (H, H), dtype=jnp.float32) * std
        Wk = jax.random.normal(k4, (H, H), dtype=jnp.float32) * std
        bq = jnp.zeros((H,), dtype=jnp.float32)
        bk = jnp.zeros((H,), dtype=jnp.float32)
        return {'inst_feature': inst_feature, 'aggregator_matrix': agg, 'rel_pair_index': rel_pair_index, 'Wq': Wq, 'bq': bq, 'Wk': Wk, 'bk': bk}
    _L0_gnn_all = _L0_gnn_setup()
    _L0_gnn_in = {k: v for k, v in _L0_gnn_all.items() if k in ('rel_pair_index', 'Wq', 'bq', 'Wk', 'bk')}
    del _L0_gnn_all

    def _L1_gnn_setup():
        import jax, jax.numpy as jnp
        import numpy as np
        N = 4096
        D = 512

        def adjacent_mat(adj):
            adj = adj + jnp.eye(adj.shape[0], dtype=adj.dtype)
            deg = jnp.sum(adj, axis=1)
            dinv = jnp.where(deg > 0, deg ** (-0.5), 0.0).astype(adj.dtype)
            return dinv[:, None] * adj * dinv[None, :]
        key = jax.random.key(seed)
        k1, k2 = jax.random.split(key)
        x = jax.random.normal(k1, (N, D), dtype=jnp.float32)
        Coefficient2 = 1e-08 * jnp.ones((N, N), dtype=jnp.float32)
        A = jax.random.uniform(k2, (N, N), dtype=jnp.float32)
        return {'x': x, 'Coefficient2': Coefficient2, 'A': A}
    _L1_gnn_all = _L1_gnn_setup()
    _L1_gnn_in = {k: v for k, v in _L1_gnn_all.items() if k in ()}
    del _L1_gnn_all
    return {'x': x, 'adj': adj, 'L0_gnn_rel_pair_index': _L0_gnn_in['rel_pair_index'], 'L0_gnn_Wq': _L0_gnn_in['Wq'], 'L0_gnn_bq': _L0_gnn_in['bq'], 'L0_gnn_Wk': _L0_gnn_in['Wk'], 'L0_gnn_bk': _L0_gnn_in['bk']}

def reference(x, adj, L0_gnn_rel_pair_index, L0_gnn_Wq, L0_gnn_bq, L0_gnn_Wk, L0_gnn_bk):
    import jax
    import jax.numpy as jnp

    def _L0_gnn_ref(inst_feature, aggregator_matrix, rel_pair_index, Wq, bq, Wk, bk):
        import jax, jax.numpy as jnp
        import numpy as np
        N, H, E, HEADS = (1500, 512, 10000, 8)
        DK = H // HEADS
        n = inst_feature.shape[0]
        sub = rel_pair_index[:, 0]
        obj = rel_pair_index[:, 1]
        q = (inst_feature[sub] @ Wq.T + bq).reshape(-1, HEADS, DK)
        k = (inst_feature[obj] @ Wk.T + bk).reshape(-1, HEADS, DK)
        att = ((q * k).sum(-1) / np.sqrt(DK)).T.astype(inst_feature.dtype)
        scores = jnp.zeros((HEADS, n, n), dtype=inst_feature.dtype)
        scores = scores.at[:, sub, obj].set(att)
        mask = (1.0 - aggregator_matrix).astype(bool)
        scores = jnp.where(mask[None], -jnp.inf, scores)
        di = jnp.arange(n)
        scores = scores.at[:, di, di].set(1e-07)
        attn = jax.nn.softmax(scores, axis=2)
        aggregator_factor = attn.sum(axis=0) / HEADS
        return aggregator_factor @ inst_feature

    def _L1_gnn_ref(x, Coefficient2, A):
        import jax, jax.numpy as jnp
        import numpy as np
        N = 4096
        D = 512

        def adjacent_mat(adj):
            adj = adj + jnp.eye(adj.shape[0], dtype=adj.dtype)
            deg = jnp.sum(adj, axis=1)
            dinv = jnp.where(deg > 0, deg ** (-0.5), 0.0).astype(adj.dtype)
            return dinv[:, None] * adj * dinv[None, :]
        A_c = jax.lax.stop_gradient(A)
        adj = adjacent_mat((A_c + A_c.T) * 0.5)
        y = Coefficient2 @ adj
        y = y @ x
        return y
    x = _layernorm(x + _L0_gnn_ref(x, adj, L0_gnn_rel_pair_index, L0_gnn_Wq, L0_gnn_bq, L0_gnn_Wk, L0_gnn_bk), axis=-1)
    x = _layernorm(x + _L1_gnn_ref(x, adj, adj), axis=-1)
    return x

_drawn_inputs = setup_inputs


def setup_inputs(seed=0):
    import zlib

    import numpy as np

    out = dict(_drawn_inputs(seed))
    spreads = {'L0_gnn_bq': (0.0, 0.8), 'L0_gnn_bk': (0.0, 0.8)}
    factors = {'L0_gnn_Wq': 4.81, 'L0_gnn_Wk': 4.595}
    for name, (base, spread) in spreads.items():
        noise = np.random.default_rng([zlib.crc32(name.encode()), seed]).standard_normal(out[name].shape)
        drawn = base * np.exp(spread * noise) if base else spread * noise
        out[name] = jnp.asarray(drawn.astype(out[name].dtype))
    for name, factor in factors.items():
        out[name] = (out[name] * factor).astype(out[name].dtype)
    return out
```

```python
import concourse.bass as bass
from concourse import mybir
from concourse.alu_op_type import AluOpType as ALU
from contextlib import ExitStack

ACT = mybir.ActivationFunctionType
AX = mybir.AxisListType
f32, bf16, f16, i32 = mybir.dt.float32, mybir.dt.bfloat16, mybir.dt.float16, mybir.dt.int32

P = 128
N, H = 1354, 512
HEADS = 8
DK = H // HEADS
E = 10000
C = -(-N // P)
NP = C * P
TAIL = N - (C - 1) * P
EC = -(-E // P)
EFULL = E // EC
EREST = E - EFULL * EC
HC = H // P
STAGES = 3
DIAG = 1e-7
EPS = 1e-5
FAR = 1e30
XS, ZS = 2048.0, 64.0
GROUP_A = list(range(0, 6))
GROUP_B = list(range(6, C))
PIECES = [(0, 4), (4, 8), (8, C)]


class Steps:

    def __init__(self, eng, sem, base=0, by=1):
        self.eng, self.sem, self.base, self.by, self.n = eng, sem, base, by, 0

    def __call__(self, instruction):
        instruction.then_inc(self.sem, self.by)
        self.n += self.by
        self.eng.wait_ge(self.sem, self.base + self.n)


LOOP1_STEPS, LOOP2_STEPS, LOOP3_STEPS, KEY_STEPS = 23, 6, 5, 5


def build(nc, x, adj_t, pairs, wq_t, bq, wk_t, bk, out):
    ctx = ExitStack()
    with ctx:
        ctx.enter_context(nc.allow_non_contiguous_dma(reason="the adjacency's diagonal"))

        def sb(name, shape, dt):
            return ctx.enter_context(nc.sbuf_tensor(name, shape, dt))

        def sem(name):
            return ctx.enter_context(nc.semaphore(name))

        at = sb("at", [P, C, NP], f16)
        bm = sb("bm", [P, C, NP], f16)
        xs = sb("xs", [P, C, H], f32)
        h = sb("h", [P, C, H], f32)
        parts = sb("parts", [P, 3 * C * H], bf16)
        stage = sb("stage", [P, STAGES * NP], f32)
        gath = sb("gath", [P, 2, H], f32)
        gath_t = sb("gath_t", [P, 2, HC, P], f32)
        biases = sb("biases", [1, 2, H], f32)

        xp = parts[:, :].rearrange("p (s c d) -> p s c d", s=3, c=C)
        words = parts[:, :].bitcast(f32)
        onehot = parts[:, 0:EC * P].bitcast(f16).rearrange("p (c s) -> p c s", s=P)
        w0 = EC * P // 2
        rows_e = words[:, w0:w0 + NP]
        rows_t = words[:, w0 + NP:w0 + 2 * NP].rearrange("p (c s) -> p c s", c=C)
        diag = words[:, 0:9 * P].rearrange("p (h s) -> p h s", h=9)
        far = words[:, 1152:1152 + 1024].rearrange("p (h s) -> p h s", h=HEADS)
        prod = words[:, 2176:2176 + H]
        k_sb = words[:, 2688:2688 + H]
        xt = parts[:, 0:2 * C * H].bitcast(f16).rearrange("p (s c d) -> p s c d", s=2, c=C)
        zt = xs[:, :, :].bitcast(f16).rearrange("p c d -> p (c d)").rearrange("p (s c d) -> p s c d", s=2, c=C)
        stg = stage[:, :].rearrange("p (s n) -> p s n", s=STAGES)
        w_sb = stage[:, 0:2 * HC * H].rearrange("p (w c n) -> p w c n", w=2, c=HC)

        ident = sb("ident", [P, P], f32)
        ident16 = sb("ident16", [P, P], f16)
        ones = sb("ones", [P, P], f32)
        ones16 = sb("ones16", [P, P], f16)
        before = sb("before", [P, P], f32)
        above16 = sb("above16", [P, P], f16)
        node_row = sb("node_row", [P, NP], f16)
        slot_row = sb("slot_row", [P, P], f16)
        node_id = sb("node_id", [P, C], f32)
        slot_id = sb("slot_id", [P, EC], f32)

        raw = sb("raw", [P, EC, 2], i32)
        pf = sb("pf", [P, EC, 2], f32)
        pg = sb("pg", [P, EC, 2], f32)
        ok = sb("ok", [P, EC], f32)
        ok2 = sb("ok2", [P, EC], f32)
        at_idx = sb("at_idx", [P, EC], i32)
        kept = sb("kept", [P, EC], f32)
        code = sb("code", [P, EC, 3], f16)
        rank = sb("rank", [P, EC], f32)
        rank16 = sb("rank16", [P, EC], f16)
        onecol = sb("onecol", [P, EC], f32)
        total16 = sb("total16", [P, 1], f16)
        base = sb("base", [P, 2], f32)
        count_i = sb("count_i", [P, 2], i32)
        tiles_i = sb("tiles_i", [P, 1], i32)

        slots = sb("slots", [P, EC, 4], f32)
        pair_key = sb("pair_key", [P, EC], f32)
        scores = sb("scores", [P, EC, HEADS], f32)
        weights = sb("weights", [P, EC, 9], f32)
        so = sb("so", [P, 4], f32)
        so_i = sb("so_i", [P, 2], i32)
        key = sb("key", [P, 2], f32)
        ahead = sb("ahead", [P, 1], f32)
        repeats = sb("repeats", [P, 2], f32)
        slot_col = sb("slot_col", [P, P], f32)
        tmp = sb("tmp", [P, 4], f32)
        same = sb("same", [P, P], f32)
        same2 = sb("same2", [P, P], f32)
        s8 = sb("s8", [P, 9], f32)
        r8 = sb("r8", [P, 9], f32)
        m_tab = sb("m_tab", [P, C, HEADS], f32)
        z_tab = sb("z_tab", [P, C, 9], f32)
        q_tab = sb("q_tab", [P, C, 9], f32)
        e_diag = sb("e_diag", [P, C, HEADS], f32)
        e_zero = sb("e_zero", [P, C, HEADS], f32)
        zz = sb("zz", [P, C, HEADS], f32)
        c_tab = sb("c_tab", [P, C], f32)
        d_tab = sb("d_tab", [P, C], f32)
        a_ii = sb("a_ii", [P, C], f32)
        row3 = sb("row3", [P, C, 3], f32)
        row_a = sb("row_a", [P, C], f32)
        deg = sb("deg", [P, C], f32)
        dinv = sb("dinv", [P, C], f32)
        dinv_x = sb("dinv_x", [P, C], f32)
        dinv_z = sb("dinv_z", [P, C], f32)
        stats = sb("stats", [P, C, 6], f32)
        mv = sb("mv", [P, C, 2], f32)
        std = sb("std", [P, C], f32)
        rstd = sb("rstd", [P, C], f32)
        nmr = sb("nmr", [P, C], f32)
        eps_c = sb("eps_c", [P, 1], f32)

        ps = ctx.enter_context(nc.psum_tensor("ps", [P, 8, 512], f32))

        pads = sem("pads")
        pairs_in = sem("pairs_in")
        x_in = sem("x_in")
        aii_in = sem("aii_in")
        bias_in = sem("bias_in")
        w_in = sem("w_in")
        stage_in = [sem(f"stage_in{i}") for i in range(STAGES)]
        at_ready = sem("at_ready")
        consts = sem("consts")
        pool_step = sem("pool_step")
        pool_passed = sem("pool_passed")
        idx_ready = sem("idx_ready")
        kept_in = sem("kept_in")
        x_first = sem("x_first")
        x_rest = sem("x_rest")
        x_second = sem("x_second")
        x_third = sem("x_third")
        ax_done = sem("ax_done")
        ax_out = sem("ax_out")
        a_piece = sem("a_piece")
        a_out = sem("a_out")
        bm_ready = sem("bm_ready")
        deg_ready = sem("deg_ready")
        root_ready = sem("root_ready")
        v_step = sem("v_step")
        v_passed = sem("v_passed")
        base_in = sem("base_in")
        base_done = sem("base_done")
        tiles_ready = sem("tiles_ready")
        l1_step = sem("l1_step")
        l1_onehot = sem("l1_onehot")
        l1_packed = sem("l1_packed")
        l1_idx = sem("l1_idx")
        key_step = sem("key_step")
        key_diag = sem("key_diag")
        key_row = sem("key_row")
        l1_sub = sem("l1_sub")
        l1_obj = sem("l1_obj")
        l1_turned = sem("l1_turned")
        l1_turned_sb = sem("l1_turned_sb")
        l1_k = sem("l1_k")
        l1_q = sem("l1_q")
        l1_k_sb = sem("l1_k_sb")
        l1_subdiag = sem("l1_subdiag")
        l1_subrow = sem("l1_subrow")
        l1_sdiag = sem("l1_sdiag")
        l1_srow = sem("l1_srow")
        l1_max = sem("l1_max")
        l1_table = sem("l1_table")
        l1_tile = sem("l1_tile")
        l2_step = sem("l2_step")
        l2_diag = sem("l2_diag")
        l2_row = sem("l2_row")
        l2_rows_t = sem("l2_rows_t")
        l2_m = sem("l2_m")
        l2_arg = sem("l2_arg")
        l2_exp = sem("l2_exp")
        l2_weights = sem("l2_weights")
        l2_table = sem("l2_table")
        l2_tile = sem("l2_tile")
        exp_arg = sem("exp_arg")
        exp_done = sem("exp_done")
        cax_in = sem("cax_in")
        cax_done = sem("cax_done")
        q_ready = sem("q_ready")
        l3_step = sem("l3_step")
        l3_obj = sem("l3_obj")
        l3_diag = sem("l3_diag")
        l3_row = sem("l3_row")
        l3_rows_t = sem("l3_rows_t")
        l3_q = sem("l3_q")
        l3_v = sem("l3_v")
        l3_done = sem("l3_done")
        l3_added = sem("l3_added")
        l3_tile = sem("l3_tile")
        var0 = sem("var0")
        std0 = sem("std0")
        x1_ready = sem("x1_ready")
        xt_hi = sem("xt_hi")
        xt_lo = sem("xt_lo")
        bx_done = sem("bx_done")
        zt_hi = sem("zt_hi")
        zt_lo = sem("zt_lo")
        y_done = sem("y_done")
        y_added = sem("y_added")
        var1 = sem("var1")
        std1 = sem("std1")
        scaled = sem("scaled")
        out_done = sem("out_done")

        x_rows = x[0:(C - 1) * P, :].rearrange("(c p) d -> p c d", p=P)
        adj_flat = adj_t.rearrange("a b -> (a b)").rearrange("(n o) -> n o", o=1)

        def loop_tiles(eng):
            eng.wait_ge(tiles_ready, 1)
            return eng.value_load(tiles_i[0:1, 0:1], min_val=1, max_val=EC)

        block = ctx.enter_context(nc.Block())

        @block.sync
        def _(sp):
            sp.wait_ge(pads, 1)
            sp.dma_start(raw[0:EFULL, :, :], pairs[0:EFULL * EC, :].rearrange("(p c) two -> p c two", c=EC)).then_inc(pairs_in, 16)
            sp.dma_start(raw[EFULL:EFULL + 1, 0:EREST, :],
                         pairs[EFULL * EC:E, :].rearrange("(p c) two -> p c two", p=1)).then_inc(pairs_in, 16)
            sp.wait_ge(pads, 4)
            sp.dma_start(xs[:, 0:C - 1, :], x_rows).then_inc(x_in, 16)
            sp.dma_start(xs[0:TAIL, C - 1, :], x[(C - 1) * P:N, :]).then_inc(x_in, 16)
            for k in range(C):
                if k >= STAGES:
                    sp.wait_ge(at_ready, k - STAGES + 1)
                rows = P if k < C - 1 else TAIL
                sp.dma_start(stg[0:rows, k % STAGES, 0:N], adj_t[k * P:k * P + rows, :]).then_inc(stage_in[k % STAGES], 16)
            sp.dma_start(a_ii[:, 0:C - 1].rearrange("p (c o) -> p c o", o=1), bass.AP(tensor=adj_t.tensor, offset=0, ap=[[N + 1, P], [P * (N + 1), C - 1], [1, 1]])).then_inc(aii_in, 16)
            sp.dma_start(a_ii[0:TAIL, C - 1:C],
                         bass.AP(tensor=adj_t.tensor, offset=(C - 1) * P * (N + 1), ap=[[N + 1, TAIL], [1, 1]])).then_inc(aii_in, 16)
            sp.dma_start(biases[0:1, 0, :], bq.rearrange("(o n) -> o n", o=1)).then_inc(bias_in, 16)
            sp.dma_start(biases[0:1, 1, :], bk.rearrange("(o n) -> o n", o=1)).then_inc(bias_in, 16)
            sp.wait_ge(at_ready, C)
            sp.dma_start(w_sb[:, 0, :, :], wq_t.rearrange("(c p) n -> p c n", p=P)).then_inc(w_in, 16)
            sp.dma_start(w_sb[:, 1, :, :], wk_t.rearrange("(c p) n -> p c n", p=P)).then_inc(w_in, 16)
            for i in range(C):
                rows = P if i < C - 1 else TAIL
                sp.wait_ge(scaled, i + 1)
                sp.dma_start(out[i * P:i * P + rows, :], h[0:rows, i, :]).then_inc(out_done, 16)
            sp.wait_ge(out_done, 16 * C)

        @block.gpsimd
        def _(pool):
            step = Steps(pool, pool_step)
            for t in (ident, ident16, before, above16):
                v = 0.0 if t in (ident, ident16) else 1.0
                pool.memset(t[:, :], v).then_inc(pool_step, 1)
                step.n += 1
            pool.wait_ge(pool_step, step.n)
            for t in (ident, ident16):
                pool.affine_select(out=t[:, :], in_=t[:, :], compare_op=ALU.not_equal, fill=1.0, base=0,
                                   pattern=[[-1, P]], channel_multiplier=1).then_inc(consts, 1)
            pool.affine_select(out=before[:, :], in_=before[:, :], compare_op=ALU.is_gt, fill=0.0, base=0,
                               pattern=[[-1, P]], channel_multiplier=1).then_inc(consts, 1)
            pool.affine_select(out=above16[:, :], in_=above16[:, :], compare_op=ALU.is_gt, fill=0.0, base=0,
                               pattern=[[1, P]], channel_multiplier=-1).then_inc(consts, 1)
            imp = dict(allow_small_or_imprecise_dtypes=True)
            pool.iota(slot_row[:, :], pattern=[[1, P]], base=1, channel_multiplier=0, **imp).then_inc(consts, 1)
            pool.iota(node_id[:, :], pattern=[[P, C]], base=0, channel_multiplier=1, **imp).then_inc(consts, 1)
            pool.iota(slot_id[:, :], pattern=[[P, EC]], base=0, channel_multiplier=1, **imp).then_inc(consts, 1)
            pool.iota(slot_col[:, :], pattern=[[1, P]], base=0, channel_multiplier=0, **imp).then_inc(consts, 1)
            pool.iota(node_row[:, :], pattern=[[1, NP]], base=0, channel_multiplier=0, **imp).then_inc(consts, 1)
            pool.wait_ge(idx_ready, 1)
            for c in range(EC):
                pool.indirect_dma_start(out=kept[:, c:c + 1], out_offset=None, in_=adj_flat,
                                        in_offset=bass.IndirectOffsetOnAxis(ap=at_idx[:, c:c + 1], axis=0)).then_inc(kept_in, 16)
            def pool_wait(signal, value):
                pool.wait_ge(signal, value)
                pool.sem_inc(pool_passed, 1)

            tiles = loop_tiles(pool)
            with pool.Fori(0, tiles) as t:
                pool_wait(l1_idx, t + 1)
                pool.indirect_dma_start(out=gath[:, 0, :], out_offset=None, in_=x,
                                        in_offset=bass.IndirectOffsetOnAxis(ap=so_i[:, 0:1], axis=0)).then_inc(l1_sub, 16)
                pool.indirect_dma_start(out=gath[:, 1, :], out_offset=None, in_=x,
                                        in_offset=bass.IndirectOffsetOnAxis(ap=so_i[:, 1:2], axis=0)).then_inc(l1_obj, 16)
                pool_wait(l1_tile, t + 1)
            with pool.Fori(0, tiles) as t:
                pool_wait(l3_diag, t + 1)
                pool.indirect_dma_start(out=gath[:, 1, :], out_offset=None, in_=x,
                                        in_offset=bass.IndirectOffsetOnAxis(ap=so_i[:, 1:2], axis=0)).then_inc(l3_obj, 16)
                pool_wait(l3_tile, t + 1)

        @block.scalar
        def _(act):
            act.wait_ge(x_in, 32)
            for k in range(C):
                act.activation(xp[:, 0, k, :], xs[:, k, :], ACT.Copy).then_inc(x_first, 1)
                act.wait_ge(x_rest, k + 1)
                act.activation(xp[:, 1, k, :], h[:, k, :], ACT.Copy).then_inc(x_second, 1)
                act.wait_ge(stage_in[k % STAGES], 16 * (k // STAGES + 1))
                rows = P if k < C - 1 else TAIL
                if k == C - 1:
                    act.wait_ge(pads, 7)
                act.activation(at[0:rows, k, 0:N], stg[0:rows, k % STAGES, 0:N], ACT.Copy).then_inc(at_ready, 1)

            def ax_evacuate(n, i, bank):
                act.wait_ge(ax_done, n + 1)
                if n == 0:
                    act.wait_ge(x_third, C)
                act.activation(h[:, i, :], ps[:, bank, :], ACT.Copy).then_inc(ax_out, 1)

            for n, i in enumerate(GROUP_A):
                ax_evacuate(n, i, i)
            for r in range(C):
                for n, (lo, hi) in enumerate(PIECES):
                    q = 3 * r + n
                    act.wait_ge(a_piece, q + 1)
                    act.activation(bm[:, r, lo * P:hi * P], ps[:, 6 + q % 2, 0:(hi - lo) * P], ACT.Copy,
                                   accum_out=row3[:, r, n:n + 1]).then_inc(a_out, 1)
            for n, i in enumerate(GROUP_B):
                ax_evacuate(len(GROUP_A) + n, i, n)
            act.wait_ge(deg_ready, 1)
            act.activation(std[:, :], deg[:, :], ACT.Sqrt).then_inc(root_ready, 1)
            tiles = loop_tiles(act)
            with act.Fori(0, tiles) as t:
                for w in range(2):
                    act.wait_ge(l1_turned, 2 * t + w + 1)
                    act.activation(gath_t[:, w, :, :], ps[:, 3 + w, :].rearrange("p (c s) -> p c s", c=HC), ACT.Copy).then_inc(l1_turned_sb, 1)
                act.wait_ge(l1_k, t + 1)
                act.activation(k_sb, ps[:, 6, :], ACT.Copy).then_inc(l1_k_sb, 1)
                act.wait_ge(l1_tile, t + 1)
            with act.Fori(0, tiles) as t:
                act.wait_ge(l2_arg, t + 1)
                act.activation(s8[:, 0:HEADS], s8[:, 0:HEADS], ACT.Exp).then_inc(l2_exp, 1)
            act.wait_ge(exp_arg, 1)
            act.activation(e_diag[:, :, :], e_diag[:, :, :], ACT.Exp).then_inc(exp_done, 1)
            act.activation(e_zero[:, :, :], m_tab[:, :, :], ACT.Exp, scale=-1.0).then_inc(exp_done, 1)
            act.wait_ge(cax_in, 1)
            for i in range(C):
                act.activation(h[:, i, :], h[:, i, :], ACT.Copy, scale=c_tab[:, i:i + 1]).then_inc(cax_done, 1)
            act.wait_ge(var0, 1)
            act.activation(std[:, :], mv[:, :, 1], ACT.Sqrt, bias=eps_c[:, 0:1]).then_inc(std0, 1)
            for i in range(C):
                act.wait_ge(x1_ready, i + 1)
                act.activation(xt[:, 0, i, :], h[:, i, :], ACT.Copy, scale=dinv_x[:, i:i + 1]).then_inc(xt_hi, 1)

            for n, i in enumerate(GROUP_A + GROUP_B):
                act.wait_ge(bx_done, n + 1)
                act.activation(zt[:, 0, i, :], ps[:, n % 8, :], ACT.Copy, scale=dinv_z[:, i:i + 1]).then_inc(zt_hi, 1)
            for i in range(C):
                act.wait_ge(var1, i + 1)
                act.activation(std[:, i:i + 1], mv[:, i, 1:2], ACT.Sqrt, bias=eps_c[:, 0:1]).then_inc(std1, 1)

        @block.tensor
        def _(pe):
            def product(group, banks, bank_free, ready, weights_of, terms, done, extra=None):
                def k_step(k, first, last):
                    ready(k)
                    for n, i in enumerate(group):
                        if first:
                            bank_free(n)
                        for s in range(len(terms)):
                            m = pe.matmul(ps[:, banks[n], :], weights_of(k, i), terms[s][:, k, :],
                                          start=first and s == 0, stop=last and s == len(terms) - 1)
                        if last:
                            m.then_inc(done, 1)
                    if extra:
                        extra(k)

                k_step(0, True, False)
                with pe.Fori(1, C - 1) as k:
                    k_step(k, False, False)
                k_step(C - 1, False, True)

            x_terms = [xp[:, s, :, :] for s in range(3)]

            def a_block(k, i):
                return at[:, k, i * P:(i + 1) * P]

            def x_and_a(k):
                pe.wait_ge(x_second, k + 1)
                pe.wait_ge(x_third, k + 1)
                pe.wait_ge(at_ready, k + 1)

            pe.wait_ge(pads, 7)
            pe.wait_ge(consts, 9)
            product(GROUP_A, GROUP_A, lambda n: None, x_and_a, a_block, x_terms, ax_done)

            for r in range(C):
                for n, (lo, hi) in enumerate(PIECES):
                    q = 3 * r + n
                    if q >= 2:
                        pe.wait_ge(a_out, q - 1)
                    for j in range(lo, hi):
                        m = pe.matmul(ps[:, 6 + q % 2, (j - lo) * P:(j - lo + 1) * P],
                                      at[:, j, r * P:(r + 1) * P], ident16[:, :], start=True, stop=True)
                    m.then_inc(a_piece, 1)

            product(GROUP_B, list(range(len(GROUP_B))), lambda n: pe.wait_ge(ax_out, n + 1), lambda k: None,
                    a_block, x_terms, ax_done)

            pe.wait_ge(base_in, 1)
            pe.matmul(ps[:, 5, 0:1], above16[:, :], total16[:, :], start=True, stop=True)
            pe.matmul(ps[:, 5, 1:2], ones16[:, :], total16[:, :], start=True, stop=True).then_inc(base_done, 1)

            tiles = loop_tiles(pe)
            with pe.Fori(0, tiles) as t:
                pe.wait_ge(l1_onehot, t + 1)
                for c in range(EC):
                    m = pe.matmul(ps[:, 2, 0:3], onehot[:, c, :], code[:, c, :], start=(c == 0), stop=(c == EC - 1))
                m.then_inc(l1_packed, 1)
                pe.wait_ge(l1_subdiag, t + 1)
                pe.matmul(ps[:, 7, 0:P], ones[:, :], diag[:, 8, :], start=True, stop=True).then_inc(l1_subrow, 1)
                with pe.Fori(0, t + 1) as u:
                    pe.wait_ge(key_diag, t * t + t + 2 * u + 2)
                    pe.matmul(ps[:, 7, P:2 * P], ones[:, :], diag[:, 8, :], start=True, stop=True).then_inc(key_row, 2)
                for w, got in enumerate((l1_sub, l1_obj)):
                    pe.wait_ge(got, 16 * t + 16)
                    for c in range(HC):
                        m = pe.transpose(ps[:, 3 + w, c * P:(c + 1) * P], gath[:, w, c * P:(c + 1) * P], ident[:, :])
                    m.then_inc(l1_turned, 1)
                pe.wait_ge(w_in, 32)
                pe.wait_ge(bias_in, 32)
                for w, done in ((1, l1_k), (0, l1_q)):
                    pe.wait_ge(l1_turned_sb, 2 * t + 2)
                    for c in range(HC):
                        pe.matmul(ps[:, 5 + w, :], gath_t[:, w, c, :], w_sb[:, w, c, :], start=(c == 0), stop=False)
                    pe.matmul(ps[:, 5 + w, :], ones[0:1, :], biases[0:1, w, :], start=False, stop=True).then_inc(done, 1)
                pe.wait_ge(l1_sdiag, t + 1)
                for g in range(2):
                    m = pe.matmul(ps[:, 3 + g, :], ones[:, :], words[:, g * 512:(g + 1) * 512], start=True, stop=True)
                m.then_inc(l1_srow, 1)
                pe.wait_ge(l1_max, t + 1)
                for c in range(C):
                    m = pe.matmul(ps[:, 2, 16 + HEADS * c:16 + HEADS * (c + 1)], rows_e[:, c * P:(c + 1) * P], r8[:, 0:HEADS], start=True, stop=True)
                m.then_inc(l1_table, 1)
                pe.wait_ge(l1_tile, t + 1)

            with pe.Fori(0, tiles) as t:
                pe.wait_ge(l2_diag, t + 1)
                pe.matmul(ps[:, 7, 0:P], ones[:, :], diag[:, 8, :], start=True, stop=True).then_inc(l2_row, 1)
                pe.wait_ge(l2_rows_t, t + 1)
                for c in range(C):
                    m = pe.matmul(ps[:, 5, 0:HEADS], rows_t[:, c, :], m_tab[:, c, :], start=(c == 0), stop=(c == C - 1))
                m.then_inc(l2_m, 1)
                pe.wait_ge(l2_weights, t + 1)
                for c in range(C):
                    m = pe.matmul(ps[:, 6, 9 * c:9 * (c + 1)], rows_e[:, c * P:(c + 1) * P], r8[:, :], start=True, stop=True)
                m.then_inc(l2_table, 1)
                pe.wait_ge(l2_tile, t + 1)

            with pe.Fori(0, tiles) as t:
                pe.wait_ge(l3_diag, t + 1)
                pe.matmul(ps[:, 7, 0:P], ones[:, :], diag[:, 8, :], start=True, stop=True).then_inc(l3_row, 1)
                pe.wait_ge(l3_rows_t, t + 1)
                for c in range(C):
                    m = pe.matmul(ps[:, 6, 0:9], rows_t[:, c, :], q_tab[:, c, :], start=(c == 0), stop=(c == C - 1))
                m.then_inc(l3_q, 1)
                pe.wait_ge(l3_v, t + 1)
                for c in range(C):
                    if c >= 6:
                        pe.wait_ge(l3_added, C * t + c - 5)
                    pe.matmul(ps[:, c % 6, :], rows_e[:, c * P:(c + 1) * P], prod, start=True, stop=True).then_inc(l3_done, 1)
                pe.wait_ge(l3_tile, t + 1)

            x1_terms = [xt[:, s, :, :] for s in range(2)]
            z_terms = [zt[:, s, :, :] for s in range(2)]

            def b_block(k, i):
                return bm[:, k, i * P:(i + 1) * P]

            pe.wait_ge(bm_ready, 1)
            order = GROUP_A + GROUP_B
            product(GROUP_A, GROUP_A, lambda n: None,
                    lambda k: pe.wait_ge(xt_lo, k + 1), b_block, x1_terms, bx_done)
            product(GROUP_B, [n % 8 for n in GROUP_B], lambda n: pe.wait_ge(zt_lo, n - 1) if n >= 2 else None,
                    lambda k: None, b_block, x1_terms, bx_done)
            product(GROUP_A, [(n + C) % 8 for n in GROUP_A],
                    lambda n: pe.wait_ge(zt_lo, n + C - 8 + 1),
                    lambda k: pe.wait_ge(zt_lo, k + 1), a_block, z_terms, y_done)
            product(GROUP_B, [(n + C) % 8 for n in GROUP_B],
                    lambda n: pe.wait_ge(y_added, n + len(GROUP_A) - 8 + 1) if n + len(GROUP_A) >= 8 else pe.wait_ge(zt_lo, C),
                    lambda k: None, a_block, z_terms, y_done)

        @block.vector
        def _(dve):
            main = Steps(dve, v_step)
            dve.memset(raw[:, :, :], N).then_inc(pads, 1)
            dve.memset(xs[:, C - 1, :], 0.0).then_inc(pads, 1)
            dve.memset(a_ii[:, :], 0.0).then_inc(pads, 1)
            dve.memset(eps_c[:, :], EPS).then_inc(pads, 1)
            dve.memset(at[:, C - 1, :], 0.0).then_inc(pads, 1)
            dve.memset(at[:, 0:C - 1, N:NP], 0.0).then_inc(pads, 1)
            dve.memset(ones[:, :], 1.0).then_inc(pads, 1)
            main(dve.memset(ones16[:, :], 1.0))
            main(dve.memset(onecol[:, :], 1.0))
            main(dve.memset(m_tab[:, :, :], DIAG))
            main(dve.memset(z_tab[:, :, :], 0.0))
            main(dve.memset(kept[:, :], 0.0))
            dve.wait_ge(pairs_in, 32)
            main(dve.tensor_copy(pf[:, :, :], raw[:, :, :]))
            main(dve.tensor_scalar(pg[:, :, :], pf[:, :, :], 0.0, float(N), ALU.is_lt, ALU.mult))
            main(dve.tensor_tensor(pf[:, :, :], pf[:, :, :], pg[:, :, :], ALU.add))
            main(dve.tensor_scalar(pg[:, :, :], pf[:, :, :], 0.0, None, ALU.is_ge))
            main(dve.scalar_tensor_tensor(pg[:, :, :], pf[:, :, :], float(N), pg[:, :, :], ALU.is_lt, ALU.mult))
            main(dve.tensor_tensor(ok[:, :], pg[:, :, 0], pg[:, :, 1], ALU.mult))
            main(dve.tensor_tensor(ok2[:, :], pf[:, :, 0], pf[:, :, 1], ALU.not_equal))
            main(dve.tensor_tensor(ok[:, :], ok[:, :], ok2[:, :], ALU.mult))
            main(dve.scalar_tensor_tensor(ok2[:, :], pf[:, :, 1], float(N), pf[:, :, 0], ALU.mult, ALU.add))
            dve.tensor_tensor(at_idx[:, :], ok2[:, :], ok[:, :], ALU.mult).then_inc(idx_ready, 1)
            main(dve.tensor_tensor(code[:, :, 0], pf[:, :, 0], ok[:, :], ALU.mult))
            main(dve.tensor_tensor(code[:, :, 1], pf[:, :, 1], ok[:, :], ALU.mult))
            main(dve.tensor_copy(code[:, :, 2], ok[:, :]))
            for k in range(C):
                dve.wait_ge(x_first, k + 1)
                dve.tensor_tensor(h[:, k, :], xs[:, k, :], xp[:, 0, k, :], ALU.subtract).then_inc(x_rest, 1)
                dve.wait_ge(x_rest, k + 1)
                dve.wait_ge(x_second, k + 1)
                dve.tensor_tensor(xp[:, 2, k, :], h[:, k, :], xp[:, 1, k, :], ALU.subtract).then_inc(x_third, 1)
            for r in range(C):
                dve.wait_ge(a_out, 3 * r + 3)
                dve.scalar_tensor_tensor(bm[:, r, :], bm[:, r, :], 1.0, at[:, r, :], ALU.mult, ALU.add,
                                         accum_out=deg[:, r:r + 1]).then_inc(v_step, 1)
                main.n += 1
            dve.wait_ge(v_step, main.n)
            on_diag = [bm[:, c, c * P:(c + 1) * P] for c in range(C)]
            for c in range(C):
                main(dve.scalar_tensor_tensor(on_diag[c], ident16[:, :], 2.0, on_diag[c], ALU.mult, ALU.add))
            dve.tensor_reduce(row_a[:, :], row3[:, :, :], AX.X, ALU.add).then_inc(bm_ready, 1)
            dve.tensor_scalar(deg[:, :], deg[:, :], 0.5, 1.0, ALU.mult, ALU.add).then_inc(deg_ready, 1)
            dve.wait_ge(root_ready, 1)
            main(dve.reciprocal(dinv[:, :], std[:, :]))
            main(dve.tensor_scalar(dinv_x[:, :], dinv[:, :], XS, None, ALU.mult))
            main(dve.tensor_scalar(dinv_z[:, :], dinv[:, :], 0.5 * ZS / XS, None, ALU.mult))
            dve.wait_ge(kept_in, 16 * EC)
            main(dve.scalar_tensor_tensor(ok[:, :], kept[:, :], 1.0, ok[:, :], ALU.is_equal, ALU.mult))
            main(dve.tensor_tensor_scan(rank[:, :], onecol[:, :], ok[:, :], 0.0, ALU.mult, ALU.add))
            dve.tensor_copy(total16[:, :], rank[:, EC - 1:EC]).then_inc(base_in, 1)
            dve.wait_ge(base_done, 1)
            main(dve.tensor_copy(base[:, :], ps[:, 5, 0:2]))
            main(dve.scalar_tensor_tensor(rank[:, :], rank[:, :], base[:, 0:1], ok[:, :], ALU.add, ALU.mult))
            main(dve.tensor_scalar(count_i[:, 0:1], base[:, 1:2], 1.0, float(P - 1), ALU.max, ALU.add))
            dve.tensor_scalar(tiles_i[:, :], count_i[:, 0:1], 7, None, ALU.logical_shift_right).then_inc(tiles_ready, 1)
            dve.wait_ge(ax_out, C)
            dve.wait_ge(consts, 9)
            tiles = loop_tiles(dve)

            with dve.Fori(0, tiles) as t:
                step = Steps(dve, l1_step, t * LOOP1_STEPS)
                step(dve.tensor_copy(rank16[:, :], rank[:, :]))
                dve.tensor_tensor(onehot, rank16[:, :].rearrange("p (c o) -> p c o", o=1).to_broadcast([P, EC, P]),
                                  slot_row[:, :].rearrange("p (o s) -> p o s", o=1).to_broadcast([P, EC, P]),
                                  ALU.is_equal).then_inc(l1_onehot, 1)
                step(dve.tensor_scalar(rank[:, :], rank[:, :], -float(P), None, ALU.add))
                dve.wait_ge(l1_packed, t + 1)
                step(dve.tensor_copy(so[:, 0:3], ps[:, 2, 0:3]))
                dve.tensor_copy(so_i[:, :], so[:, 0:2]).then_inc(l1_idx, 1)
                step(dve.tensor_scalar(tmp[:, 2:3], so[:, 0:1], so[:, 2:3], None, ALU.add))
                step(dve.tensor_scalar(so[:, 3:4], tmp[:, 2:3], -1.0, None, ALU.add))
                dve.tensor_scalar(diag[:, 8, :], ident[:, :], so[:, 3:4], None, ALU.mult).then_inc(l1_subdiag, 1)
                step(dve.scalar_tensor_tensor(key[:, 0:1], so[:, 0:1], float(N), so[:, 1:2], ALU.mult, ALU.add))
                step(dve.tensor_copy(pair_key[:, bass.ds(t, 1)], key[:, 0:1]))
                step(dve.tensor_scalar(rows_e, node_row[:, :], so[:, 3:4], None, ALU.is_equal))
                dve.wait_ge(l1_subrow, t + 1)
                step(dve.tensor_scalar(same[:, :], ps[:, 7, 0:P], so[:, 3:4], None, ALU.is_equal))
                step(dve.tensor_tensor(same2[:, :], same[:, :], before[:, :], ALU.mult))
                step(dve.tensor_reduce(tmp[:, 3:4], same2[:, :], AX.X, ALU.add))
                step(dve.tensor_scalar(tmp[:, 2:3], tmp[:, 3:4], 0.0, None, ALU.is_equal))
                step(dve.tensor_scalar(same[:, :], same[:, :], -1.0, FAR, ALU.add, ALU.mult))
                step(dve.tensor_copy(ahead[:, :], slot_id[:, bass.ds(t, 1)]))
                step(dve.memset(repeats[:, :], 0.0))
                dve.sem_inc(v_passed, 1)
                with dve.Fori(0, t + 1) as u:
                    one = Steps(dve, key_step, (t * t + t) * KEY_STEPS + u * 2 * KEY_STEPS, by=2)
                    one(dve.tensor_copy(key[:, 1:2], pair_key[:, bass.ds(u, 1)]))
                    dve.tensor_scalar(diag[:, 8, :], ident[:, :], key[:, 1:2], None, ALU.mult).then_inc(key_diag, 2)
                    dve.wait_ge(key_row, t * t + t + 2 * u + 2)
                    one(dve.tensor_scalar(same2[:, :], ps[:, 7, P:2 * P], key[:, 0:1], None, ALU.is_equal))
                    one(dve.scalar_tensor_tensor(same2[:, :], slot_col[:, :], ahead[:, :], same2[:, :], ALU.is_lt, ALU.mult,
                                                 accum_out=repeats[:, 1:2]))
                    one(dve.tensor_tensor(repeats[:, 0:1], repeats[:, 0:1], repeats[:, 1:2], ALU.add))
                    one(dve.tensor_scalar(ahead[:, :], ahead[:, :], -float(P), None, ALU.add))
                    assert one.n == 2 * KEY_STEPS
                step(dve.scalar_tensor_tensor(so[:, 2:3], repeats[:, 0:1], 0.0, so[:, 2:3], ALU.is_equal, ALU.mult))
                step(dve.tensor_copy(slots[:, bass.ds(t, 1), :].rearrange("p o f -> p (o f)"), so[:, :]))
                dve.wait_ge(l1_q, t + 1)
                dve.wait_ge(l1_k_sb, t + 1)
                step(dve.tensor_tensor(prod, ps[:, 5, :], k_sb, ALU.mult))
                step(dve.tensor_reduce(s8[:, 0:HEADS], prod.rearrange("p (h d) -> p h d", h=HEADS), AX.X, ALU.add))
                step(dve.tensor_scalar(s8[:, 0:HEADS], s8[:, 0:HEADS], 1.0 / float(DK) ** 0.5, None, ALU.mult))
                dve.tensor_tensor(diag[:, 0:HEADS, :], ident[:, :].rearrange("p (o s) -> p o s", o=1).to_broadcast([P, HEADS, P]),
                                  s8[:, 0:HEADS].rearrange("p (h o) -> p h o", o=1).to_broadcast([P, HEADS, P]),
                                  ALU.mult).then_inc(l1_sdiag, 1)
                dve.tensor_copy(scores[:, bass.ds(t, 1), :].rearrange("p o f -> p (o f)"), s8[:, 0:HEADS]).then_inc(l1_step, 1)
                step.n += 1
                dve.wait_ge(l1_srow, t + 1)
                step(dve.tensor_tensor(far, ps[:, 3:5, :].rearrange("p b (h s) -> p (b h) s", s=P),
                                       same[:, :].rearrange("p (o s) -> p o s", o=1).to_broadcast([P, HEADS, P]), ALU.add))
                step(dve.tensor_reduce(r8[:, 0:HEADS], far, AX.X, ALU.max))
                dve.tensor_scalar(r8[:, 0:HEADS], r8[:, 0:HEADS], tmp[:, 2:3], None, ALU.mult).then_inc(l1_max, 1)
                dve.wait_ge(l1_table, t + 1)
                dve.tensor_tensor(m_tab[:, :, :], m_tab[:, :, :],
                                  ps[:, 2, 16:16 + HEADS * C].rearrange("p (c h) -> p c h", c=C), ALU.max).then_inc(l1_tile, 1)
                assert step.n == LOOP1_STEPS, step.n
                dve.wait_ge(l1_tile, t + 1)

            with dve.Fori(0, tiles) as t:
                step = Steps(dve, l2_step, t * LOOP2_STEPS)
                step(dve.tensor_copy(so[:, :], slots[:, bass.ds(t, 1), :].rearrange("p o f -> p (o f)")))
                dve.tensor_scalar(diag[:, 8, :], ident[:, :], so[:, 3:4], None, ALU.mult).then_inc(l2_diag, 1)
                step(dve.tensor_scalar(rows_e, node_row[:, :], so[:, 3:4], None, ALU.is_equal))
                step(dve.tensor_copy(s8[:, 0:HEADS], scores[:, bass.ds(t, 1), :].rearrange("p o f -> p (o f)")))
                dve.wait_ge(l2_row, t + 1)
                dve.tensor_tensor(rows_t, ps[:, 7, 0:P].rearrange("p (o s) -> p o s", o=1).to_broadcast([P, C, P]),
                                  node_id[:, :].rearrange("p (c o) -> p c o", o=1).to_broadcast([P, C, P]),
                                  ALU.is_equal).then_inc(l2_rows_t, 1)
                dve.wait_ge(l2_m, t + 1)
                step(dve.tensor_tensor(s8[:, 0:HEADS], s8[:, 0:HEADS], ps[:, 5, 0:HEADS], ALU.subtract))
                dve.tensor_scalar(s8[:, 0:HEADS], s8[:, 0:HEADS], so[:, 2:3], None, ALU.mult).then_inc(l2_arg, 1)
                dve.wait_ge(l2_exp, t + 1)
                step(dve.tensor_scalar(r8[:, 0:HEADS], s8[:, 0:HEADS], so[:, 2:3], None, ALU.mult))
                dve.tensor_copy(r8[:, 8:9], so[:, 2:3]).then_inc(l2_weights, 1)
                dve.wait_ge(l2_weights, t + 1)
                step(dve.tensor_copy(weights[:, bass.ds(t, 1), :].rearrange("p o f -> p (o f)"), r8[:, :]))
                dve.wait_ge(l2_table, t + 1)
                dve.tensor_tensor(z_tab[:, :, :], z_tab[:, :, :],
                                  ps[:, 6, 0:9 * C].rearrange("p (c h) -> p c h", c=C), ALU.add).then_inc(l2_tile, 1)
                assert step.n == LOOP2_STEPS, step.n
                dve.wait_ge(l2_tile, t + 1)

            dve.tensor_scalar(e_diag[:, :, :], m_tab[:, :, :], -1.0, DIAG, ALU.mult, ALU.add).then_inc(exp_arg, 1)
            dve.wait_ge(aii_in, 32)
            main(dve.tensor_tensor(row_a[:, :], row_a[:, :], a_ii[:, :], ALU.subtract))
            main(dve.tensor_tensor(row_a[:, :], row_a[:, :], z_tab[:, :, 8], ALU.subtract))
            dve.wait_ge(exp_done, 2)
            main(dve.tensor_tensor(zz[:, :, :], e_zero[:, :, :],
                                   row_a[:, :].rearrange("p (c o) -> p c o", o=1).to_broadcast([P, C, HEADS]), ALU.mult))
            main(dve.tensor_tensor(zz[:, :, :], zz[:, :, :], e_diag[:, :, :], ALU.add))
            main(dve.tensor_tensor(zz[:, :, :], zz[:, :, :], z_tab[:, :, 0:HEADS], ALU.add))
            main(dve.reciprocal(zz[:, :, :], zz[:, :, :]))
            main(dve.tensor_scalar(q_tab[:, :, 0:HEADS], zz[:, :, :], 1.0 / HEADS, None, ALU.mult))
            main(dve.tensor_tensor(e_zero[:, :, :], e_zero[:, :, :], q_tab[:, :, 0:HEADS], ALU.mult))
            main(dve.tensor_tensor(e_diag[:, :, :], e_diag[:, :, :], q_tab[:, :, 0:HEADS], ALU.mult))
            main(dve.tensor_reduce(c_tab[:, :], e_zero[:, :, :], AX.X, ALU.add))
            dve.tensor_scalar(q_tab[:, :, 8], c_tab[:, :], -1.0, None, ALU.mult).then_inc(cax_in, 1)
            main(dve.tensor_reduce(d_tab[:, :], e_diag[:, :, :], AX.X, ALU.add))
            main(dve.tensor_tensor(a_ii[:, :], a_ii[:, :], c_tab[:, :], ALU.mult))
            main(dve.scalar_tensor_tensor(d_tab[:, :], d_tab[:, :], 1.0, a_ii[:, :], ALU.add, ALU.subtract))
            for i in range(C):
                dve.wait_ge(cax_done, i + 1)
                dve.scalar_tensor_tensor(h[:, i, :], xs[:, i, :], d_tab[:, i:i + 1], h[:, i, :], ALU.mult, ALU.add).then_inc(v_step, 1)
                main.n += 1
            dve.wait_ge(v_step, main.n)

            with dve.Fori(0, tiles) as t:
                step = Steps(dve, l3_step, t * LOOP3_STEPS)
                step(dve.tensor_copy(so[:, :], slots[:, bass.ds(t, 1), :].rearrange("p o f -> p (o f)")))
                step(dve.tensor_copy(so_i[:, :], so[:, 0:2]))
                dve.tensor_scalar(diag[:, 8, :], ident[:, :], so[:, 3:4], None, ALU.mult).then_inc(l3_diag, 1)
                step(dve.tensor_scalar(rows_e, node_row[:, :], so[:, 3:4], None, ALU.is_equal))
                dve.wait_ge(l3_row, t + 1)
                dve.tensor_tensor(rows_t, ps[:, 7, 0:P].rearrange("p (o s) -> p o s", o=1).to_broadcast([P, C, P]),
                                  node_id[:, :].rearrange("p (c o) -> p c o", o=1).to_broadcast([P, C, P]),
                                  ALU.is_equal).then_inc(l3_rows_t, 1)
                dve.wait_ge(l3_q, t + 1)
                step(dve.tensor_tensor(r8[:, :], ps[:, 6, 0:9], weights[:, bass.ds(t, 1), :].rearrange("p o f -> p (o f)"), ALU.mult))
                step(dve.tensor_reduce(tmp[:, 0:1], r8[:, :], AX.X, ALU.add))
                dve.wait_ge(l3_obj, 16 * t + 16)
                dve.tensor_scalar(prod, gath[:, 1, :], tmp[:, 0:1], None, ALU.mult).then_inc(l3_v, 1)
                for c in range(C):
                    dve.wait_ge(l3_done, C * t + c + 1)
                    dve.tensor_tensor(h[:, c, :], h[:, c, :], ps[:, c % 6, :], ALU.add).then_inc(l3_added, 1)
                dve.wait_ge(l3_added, C * t + C)
                assert step.n == LOOP3_STEPS, step.n
                dve.sem_inc(l3_tile, 1)

            for i in range(C):
                dve.bn_stats(stats[:, i, :], h[:, i, :]).then_inc(v_step, 1)
                main.n += 1
                dve.wait_ge(v_step, main.n)
                dve.bn_aggr(mv[:, i, :], stats[:, i, :]).then_inc(v_step, 1)
                main.n += 1
            dve.wait_ge(v_step, main.n)
            dve.sem_inc(var0, 1)
            dve.wait_ge(std0, 1)
            main(dve.reciprocal(rstd[:, :], std[:, :]))
            for i in range(C):
                dve.tensor_scalar(h[:, i, :], h[:, i, :], mv[:, i, 0:1], rstd[:, i:i + 1], ALU.subtract, ALU.mult).then_inc(x1_ready, 1)
                dve.wait_ge(x1_ready, i + 1)
                dve.wait_ge(xt_hi, i + 1)
                dve.scalar_tensor_tensor(xt[:, 1, i, :], h[:, i, :], dinv_x[:, i:i + 1], xt[:, 0, i, :],
                                         ALU.mult, ALU.subtract).then_inc(xt_lo, 1)
            for n, i in enumerate(GROUP_A + GROUP_B):
                dve.wait_ge(zt_hi, n + 1)
                dve.scalar_tensor_tensor(zt[:, 1, i, :], ps[:, n % 8, :], dinv_z[:, i:i + 1], zt[:, 0, i, :],
                                         ALU.mult, ALU.subtract).then_inc(zt_lo, 1)
            for n, i in enumerate(GROUP_A + GROUP_B):
                dve.wait_ge(y_done, n + 1)
                dve.scalar_tensor_tensor(h[:, i, :], ps[:, (n + C) % 8, :], 1.0 / ZS, h[:, i, :],
                                         ALU.mult, ALU.add).then_inc(y_added, 1)
                dve.wait_ge(y_added, n + 1)
                main(dve.bn_stats(stats[:, i, :], h[:, i, :]))
                dve.bn_aggr(mv[:, i, :], stats[:, i, :]).then_inc(var1, 1)
                dve.wait_ge(std1, n + 1)
                main(dve.reciprocal(rstd[:, i:i + 1], std[:, i:i + 1]))
                dve.tensor_scalar(h[:, i, :], h[:, i, :], mv[:, i, 0:1], rstd[:, i:i + 1],
                                  ALU.subtract, ALU.mult).then_inc(scaled, 1)


def kernel(x, adj, L0_gnn_rel_pair_index, L0_gnn_Wq, L0_gnn_bq, L0_gnn_Wk, L0_gnn_bk):
    import numpy as np
    import concourse.bacc as bacc
    from concourse.bass_utils import run_bass_kernel_spmd

    laid_out = {
        "x": np.ascontiguousarray(x),
        "adj_t": np.ascontiguousarray(np.asarray(adj).T),
        "pairs": np.ascontiguousarray(L0_gnn_rel_pair_index),
        "wq_t": np.ascontiguousarray(np.asarray(L0_gnn_Wq).T),
        "bq": np.ascontiguousarray(L0_gnn_bq),
        "wk_t": np.ascontiguousarray(np.asarray(L0_gnn_Wk).T),
        "bk": np.ascontiguousarray(L0_gnn_bk),
    }
    nc = bacc.Bacc("TRN2", target_bir_lowering=False, num_devices=1)
    args = [nc.dram_tensor(f"in_{k}", a.shape, mybir.dt.from_np(a.dtype), kind="ExternalInput").ap() for k, a in laid_out.items()]
    out = nc.dram_tensor("out", (N, H), f32, kind="ExternalOutput").ap()
    build(nc, *args, out)
    r = run_bass_kernel_spmd(nc, [{f"in_{k}": a for k, a in laid_out.items()}], core_ids=[0])
    return r.results[0]["out"]
```

```python
import concourse.bass as bass
from concourse import mybir
from concourse.alu_op_type import AluOpType as ALU
from contextlib import ExitStack
import numpy as np

ACT = mybir.ActivationFunctionType
AX = mybir.AxisListType
f32, bf16, f16, i32 = mybir.dt.float32, mybir.dt.bfloat16, mybir.dt.float16, mybir.dt.int32

P = 128
N, H = 1354, 512
HEADS = 8
DK = H // HEADS
E = 10000
C = -(-N // P)
NP = C * P
TAIL = N - (C - 1) * P
EC = -(-E // P)
EFULL = E // EC
EREST = E - EFULL * EC
HC = H // P
STAGES = 3
DIAG = 1e-7
EPS = 1e-5
E_ZERO = float(np.exp(-DIAG))
FAR = 1e30
XS, ZS = 2048.0, 64.0
EXPONENT = 0x7F800000
TOP = 127 + 14 + 127
GROUP_A = list(range(0, 6))
GROUP_B = list(range(6, C))
HALF = 6
PIECES = [(0, 4), (4, 8), (8, C)]
BLOCK = 16
ECP = -(-EC // BLOCK) * BLOCK
HU = H + 3
BATCH = 3
BATCHES = [(b, min(b + BATCH, C)) for b in range(0, C, BATCH)]
PARTS = [(0, 2 * BATCH), (2 * BATCH, 3 * BATCH), (3 * BATCH, C)]
AHEAD = list(range(0, 4))
BESIDE = list(range(4, C))
IN_LOOP2, IN_LOOP3, IN_LOOP4 = 2, 2, 1
SUB, OBJ, USED, SUB1, KEY = range(5)
EX_S, EX_0, EX_D, EX_ONE, EX_FIRST, EX_N = 0, HEADS, 2 * HEADS, 3 * HEADS, 3 * HEADS + 1, 3 * HEADS + 2


class Steps:

    def __init__(self, eng, sem, base=0, by=1):
        self.eng, self.sem, self.base, self.by, self.n = eng, sem, base, by, 0

    def __call__(self, instruction):
        instruction.then_inc(self.sem, self.by)
        self.n += self.by
        self.eng.wait_ge(self.sem, self.base + self.n)


PACK_STEPS, SCORE_STEPS, LOOP2_STEPS, ROW_STEPS, LOOP3_STEPS, SUM_STEPS = 5, 3, 12, 12, 17, 3
LOOP4_STEPS, TOTAL_STEPS = 15, 2


def build(nc, x, adj_t, pairs, wq_t, bq, wk_t, bk, out):
    ctx = ExitStack()
    with ctx:
        ctx.enter_context(nc.allow_non_contiguous_dma(reason="the adjacency's diagonal"))

        def sb(name, shape, dt):
            return ctx.enter_context(nc.sbuf_tensor(name, shape, dt))

        def sem(name):
            return ctx.enter_context(nc.semaphore(name))

        at = sb("at", [P, C, NP], f16)
        bm = sb("bm", [P, C, NP], f16)
        xs = sb("xs", [P, C, H], f32)
        u = sb("u", [P, C, HU], f32)
        terms = sb("terms", [P, 2, C, H], f16)
        work = sb("work", [P, ECP * P], f16)
        stage = sb("stage", [P, STAGES * NP], f32)
        gath = sb("gath", [P, 2, H], f32)
        gath_u = sb("gath_u", [P, HU], f32)
        gath_t = sb("gath_t", [P, 2, HC, P], f32)
        biases = sb("biases", [1, 2, H], f32)
        slot_cols = sb("slot_cols", [P, P, BLOCK], f16)
        rank16 = sb("rank16", [P, ECP], f16)
        dz = sb("dz", [P, 2, H], f16)

        onehot = work[:, :].rearrange("p (b s c) -> p b s c", s=P, c=BLOCK)
        words = work[:, :].bitcast(f32)
        diag = words[:, 0:10 * P].rearrange("p (h s) -> p h s", h=10)
        far = words[:, 10 * P:18 * P].rearrange("p (h s) -> p h s", h=HEADS)
        prod = words[:, 18 * P:18 * P + H]
        k_sb = words[:, 18 * P + H:18 * P + 2 * H]
        v_other = words[:, 18 * P + 2 * H:18 * P + 3 * H]
        row_x = words[:, 18 * P + 3 * H:18 * P + 4 * H]
        row_x0 = words[:, 18 * P + 4 * H:18 * P + 5 * H]
        stg = stage[:, :].rearrange("p (s n) -> p s n", s=STAGES)
        w_sb = stage[:, 0:2 * HC * H].rearrange("p (w c n) -> p w c n", w=2, c=HC)

        bm_e = stage[:, 0:NP // 2].bitcast(f16)

        ident = sb("ident", [P, P], f32)
        ident16 = sb("ident16", [P, P], f16)
        ones = sb("ones", [P, P], f32)
        ones16 = sb("ones16", [P, P], f16)
        above16 = sb("above16", [P, P], f16)
        slot_row = sb("slot_row", [P, P], f16)
        slot_id = sb("slot_id", [P, EC], f32)

        raw = sb("raw", [P, EC, 2], i32)
        pf = sb("pf", [P, EC, 2], f32)
        pg = sb("pg", [P, EC, 2], f32)
        ok = sb("ok", [P, EC], f32)
        ok2 = sb("ok2", [P, EC], f32)
        at_idx = sb("at_idx", [P, EC], i32)
        kept = sb("kept", [P, EC], f32)
        code = sb("code", [P, EC, 3], f16)
        rank = sb("rank", [P, EC], f32)
        onecol = sb("onecol", [P, EC], f32)
        total16 = sb("total16", [P, 1], f16)
        base = sb("base", [P, 2], f32)
        count_i = sb("count_i", [P, 2], i32)
        tiles_i = sb("tiles_i", [P, 1], i32)

        slots = sb("slots", [P, EC, 5], f32)
        scores = sb("scores", [P, EC, HEADS], f32)
        exps = sb("exps", [P, EC, EX_N], f32)
        so = sb("so", [P, 5], f32)
        so_i = sb("so_i", [P, 2], i32)
        other = sb("other", [P, 2], f32)
        ahead = sb("ahead", [P, 1], f32)
        earlier = sb("earlier", [P, 4], f32)
        slot_col = sb("slot_col", [P, P], f32)
        same = sb("same", [P, P], f32)
        same_row = sb("same_row", [P, P], f32)
        same_key = sb("same_key", [P, P], f32)
        s8 = sb("s8", [P, HEADS], f32)
        s_other = sb("s_other", [P, HEADS], f32)
        m8 = sb("m8", [P, HEADS], f32)
        m_new = sb("m_new", [P, HEADS], f32)
        ex = sb("ex", [P, EX_N], f32)
        ex_other = sb("ex_other", [P, EX_N], f32)
        z_sum = sb("z_sum", [P, EX_N], f32)
        zz = sb("zz", [P, HEADS], f32)
        shares = sb("shares", [P, 3, HEADS], f32)
        wcd = sb("wcd", [P, 3], f32)
        coef = sb("coef", [P, 5], f32)
        change = sb("change", [P, EC, 1], f32)
        spot = sb("spot", [P, 3], f32)
        spot_i = sb("spot_i", [P, 1], i32)
        one_z = sb("one_z", [P, C], f32)
        ratio = sb("ratio", [P, C], f32)
        a_ii = sb("a_ii", [P, C], f32)
        row3 = sb("row3", [P, C, 3], f32)
        row_a = sb("row_a", [P, C], f32)
        col_a = sb("col_a", [P, C], f32)
        squares = sb("squares", [P, 2, C], f32)
        roots = sb("roots", [P, 2, C], f32)
        inverse = sb("inverse", [P, 2, C], f32)
        dinv_x = sb("dinv_x", [P, C], f32)
        dinv_z = sb("dinv_z", [P, C], f32)
        peak = sb("peak", [P, 4], f32)
        peak_i = sb("peak_i", [1, 4], i32)
        scale = sb("scale", [P, 2], f32)
        stats = sb("stats", [P, C, 6], f32)
        mv = sb("mv", [P, C, 2], f32)
        std = sb("std", [P, C], f32)
        rstd = sb("rstd", [P, C], f32)
        nmr = sb("nmr", [P, C], f32)
        warm = sb("warm", [P, 1], f32)
        eps_c = sb("eps_c", [P, 1], f32)

        ps = ctx.enter_context(nc.psum_tensor("ps", [P, 8, 512], f32))

        u_rows = nc.dram_tensor("u_rows", [N, HU], f32).ap()
        bm_rows = nc.dram_tensor("bm_rows", [N, NP], f16).ap()
        x1_rows = nc.dram_tensor("x1_rows", [N + P, H], f32).ap()
        v_rows = nc.dram_tensor("v_rows", [EC * P, H], f32).ap()

        pads = sem("pads")
        pairs_in = sem("pairs_in")
        x_in = [sem("x_in0"), sem("x_in1")]
        aii_in = sem("aii_in")
        bias_in = sem("bias_in")
        w_in = sem("w_in")
        stage_in = [sem(f"stage_in{i}") for i in range(STAGES)]
        at_even = sem("at_even")
        at_odd = sem("at_odd")
        consts = sem("consts")
        pool_step = sem("pool_step")
        pool_passed = sem("pool_passed")
        idx_ready = sem("idx_ready")
        kept_in = sem("kept_in")
        peak_found = sem("peak_found")
        peak_row = sem("peak_row")
        scale_found = sem("scale_found")
        scale_row = sem("scale_row")
        scale_ready = sem("scale_ready")
        x_hi = sem("x_hi")
        x_lo = sem("x_lo")
        ax_done = sem("ax_done")
        ax_out = sem("ax_out")
        a_piece = sem("a_piece")
        piece_free = sem("piece_free")
        bm_ready = sem("bm_ready")
        deg_ready = sem("deg_ready")
        root_ready = sem("root_ready")
        v_step = sem("v_step")
        v_passed = sem("v_passed")
        base_in = sem("base_in")
        base_done = sem("base_done")
        tiles_ready = sem("tiles_ready")
        counts_ready = sem("counts_ready")
        u_stored = sem("u_stored")
        bm_row = sem("bm_row")
        bm_stored = sem("bm_stored")
        x1_stored = sem("x1_stored")
        l1_step = sem("l1_step")
        score_step = sem("score_step")
        l1_onehot = sem("l1_onehot")
        l1_packed = sem("l1_packed")
        l1_slots = sem("l1_slots")
        idx_taken = sem("idx_taken")
        l1_sub = sem("l1_sub")
        l1_obj = sem("l1_obj")
        l1_turned = sem("l1_turned")
        l1_turned_sb = sem("l1_turned_sb")
        l1_k = sem("l1_k")
        l1_q = sem("l1_q")
        l1_k_sb = sem("l1_k_sb")
        l1_tile = sem("l1_tile")
        l2_step = sem("l2_step")
        row_step = sem("row_step")
        id_diag = sem("id_diag")
        id_row = sem("id_row")
        s_diag = sem("s_diag")
        s_row = sem("s_row")
        l2_arg = sem("l2_arg")
        l2_exp = sem("l2_exp")
        l3_step = sem("l3_step")
        sum_step = sem("sum_step")
        l3_diag = sem("l3_diag")
        l3_row = sem("l3_row")
        l3_same = sem("l3_same")
        l3_sum = sem("l3_sum")
        l3_sub = sem("l3_sub")
        l3_obj = sem("l3_obj")
        l3_u = sem("l3_u")
        l3_tile = sem("l3_tile")
        v_stored = sem("v_stored")
        prod_free = sem("prod_free")
        l4_step = sem("l4_step")
        total_step = sem("total_step")
        l4_diag = sem("l4_diag")
        l4_row = sem("l4_row")
        l4_same = sem("l4_same")
        l4_v = sem("l4_v")
        l4_sum = sem("l4_sum")
        l4_var = sem("l4_var")
        l4_root = sem("l4_root")
        l4_x1 = sem("l4_x1")
        l4_x0 = sem("l4_x0")
        l4_bm = sem("l4_bm")
        l4_dz = sem("l4_dz")
        l4_done = sem("l4_done")
        l4_added = sem("l4_added")
        l4_tile = sem("l4_tile")
        last_done = sem("last_done")
        last_added = sem("last_added")
        x1_fixed = sem("x1_fixed")
        row_free = sem("row_free")
        var0 = sem("var0")
        std0 = sem("std0")
        nmr_ready = sem("nmr_ready")
        bx_out = sem("bx_out")
        x1_in = sem("x1_in")
        s_passed = sem("s_passed")
        x1_ready = sem("x1_ready")
        xt_hi = sem("xt_hi")
        xt_lo = sem("xt_lo")
        bx_done = sem("bx_done")
        zt_hi = sem("zt_hi")
        zt_lo = sem("zt_lo")
        y_done = sem("y_done")
        warmed = sem("warmed")
        y_added = sem("y_added")
        var1 = sem("var1")
        std1 = sem("std1")
        scaled = sem("scaled")
        out_done = sem("out_done")

        x_rows = x[0:(C - 1) * P, :].rearrange("(c p) d -> p c d", p=P)
        adj_flat = adj_t.rearrange("a b -> (a b)").rearrange("(n o) -> n o", o=1)

        def loop_tiles(eng):
            eng.wait_ge(tiles_ready, 1)
            return eng.value_load(tiles_i[0:1, 0:1], min_val=1, max_val=EC)

        block = ctx.enter_context(nc.Block())

        @block.sync
        def _(sp):
            sp.wait_ge(pads, 1)
            sp.dma_start(raw[0:EFULL, :, :], pairs[0:EFULL * EC, :].rearrange("(p c) two -> p c two", c=EC)).then_inc(pairs_in, 16)
            sp.dma_start(raw[EFULL:EFULL + 1, 0:EREST, :],
                         pairs[EFULL * EC:E, :].rearrange("(p c) two -> p c two", p=1)).then_inc(pairs_in, 16)
            sp.wait_ge(pads, 5)
            sp.dma_start(xs[:, 0:HALF, :], x_rows[:, 0:HALF, :]).then_inc(x_in[0], 16)
            sp.dma_start(xs[:, HALF:C - 1, :], x_rows[:, HALF:C - 1, :]).then_inc(x_in[1], 16)
            sp.dma_start(xs[0:TAIL, C - 1, :], x[(C - 1) * P:N, :]).then_inc(x_in[1], 16)
            for k in range(C):
                if k >= STAGES:
                    j = k - STAGES
                    sp.wait_ge(at_odd if j % 2 else at_even, j // 2 + 1)
                rows = P if k < C - 1 else TAIL
                sp.dma_start(stg[0:rows, k % STAGES, 0:N], adj_t[k * P:k * P + rows, :]).then_inc(stage_in[k % STAGES], 16)
            sp.dma_start(a_ii[:, 0:C - 1].rearrange("p (c o) -> p c o", o=1), bass.AP(tensor=adj_t.tensor, offset=0, ap=[[N + 1, P], [P * (N + 1), C - 1], [1, 1]])).then_inc(aii_in, 16)
            sp.dma_start(a_ii[0:TAIL, C - 1:C],
                         bass.AP(tensor=adj_t.tensor, offset=(C - 1) * P * (N + 1), ap=[[N + 1, TAIL], [1, 1]])).then_inc(aii_in, 16)
            sp.dma_start(biases[0:1, 0, :], bq.rearrange("(o n) -> o n", o=1)).then_inc(bias_in, 16)
            sp.dma_start(biases[0:1, 1, :], bk.rearrange("(o n) -> o n", o=1)).then_inc(bias_in, 16)
            sp.wait_ge(at_even, (C + 1) // 2)
            sp.wait_ge(at_odd, C // 2)
            sp.dma_start(w_sb[:, 0, :, :], wq_t.rearrange("(c p) n -> p c n", p=P)).then_inc(w_in, 16)
            sp.dma_start(w_sb[:, 1, :, :], wk_t.rearrange("(c p) n -> p c n", p=P)).then_inc(w_in, 16)
            for m, (lo, hi) in enumerate(PARTS):
                for i in range(lo, hi):
                    rows = P if i < C - 1 else TAIL
                    sp.wait_ge(bm_row, i + 1)
                    sp.dma_start(bm_rows[i * P:i * P + rows, :], bm[0:rows, i, :]).then_inc(bm_stored, 16)
                sp.wait_ge(counts_ready, m + 1)
                for i in range(lo, hi):
                    rows = P if i < C - 1 else TAIL
                    sp.dma_start(u_rows[i * P:i * P + rows, :], u[0:rows, i, :]).then_inc(u_stored, 16)
                for i in range(lo, hi):
                    rows = P if i < C - 1 else TAIL
                    sp.wait_ge(x1_ready, i + 1)
                    sp.dma_start(x1_rows[i * P:i * P + rows, :], xs[0:rows, i, :]).then_inc(x1_stored, 16)
            tiles = loop_tiles(sp)
            sp.wait_ge(x1_fixed, tiles * 16)
            sp.sem_inc(s_passed, 1)
            sp.wait_ge(xt_lo, C)
            for i in range(C):
                rows = P if i < C - 1 else TAIL
                sp.dma_start(xs[0:rows, i, :], x1_rows[i * P:i * P + rows, :]).then_inc(x1_in, 16)
            for i in range(C):
                rows = P if i < C - 1 else TAIL
                sp.wait_ge(scaled, i + 1)
                sp.dma_start(out[i * P:i * P + rows, :], xs[0:rows, i, :]).then_inc(out_done, 16)
            sp.wait_ge(out_done, 16 * C)

        @block.gpsimd
        def _(pool):
            step = Steps(pool, pool_step)
            for t in (ident, ident16, above16):
                v = 1.0 if t is above16 else 0.0
                pool.memset(t[:, :], v).then_inc(pool_step, 1)
                step.n += 1
            pool.wait_ge(pool_step, step.n)
            for t in (ident, ident16):
                pool.affine_select(out=t[:, :], in_=t[:, :], compare_op=ALU.not_equal, fill=1.0, base=0,
                                   pattern=[[-1, P]], channel_multiplier=1).then_inc(consts, 1)
            pool.affine_select(out=above16[:, :], in_=above16[:, :], compare_op=ALU.is_gt, fill=0.0, base=0,
                               pattern=[[1, P]], channel_multiplier=-1).then_inc(consts, 1)
            imp = dict(allow_small_or_imprecise_dtypes=True)
            pool.iota(slot_row[:, :], pattern=[[1, P]], base=1, channel_multiplier=0, **imp).then_inc(consts, 1)
            pool.iota(slot_id[:, :], pattern=[[P, EC]], base=0, channel_multiplier=1, **imp).then_inc(consts, 1)
            pool.iota(slot_col[:, :], pattern=[[1, P]], base=0, channel_multiplier=0, **imp).then_inc(consts, 1)
            pool.wait_ge(idx_ready, 1)
            for c in range(EC):
                pool.indirect_dma_start(out=kept[:, c:c + 1], out_offset=None, in_=adj_flat,
                                        in_offset=bass.IndirectOffsetOnAxis(ap=at_idx[:, c:c + 1], axis=0)).then_inc(kept_in, 16)
            def pool_wait(signal, value):
                pool.wait_ge(signal, value)
                pool.sem_inc(pool_passed, 1)

            tiles = loop_tiles(pool)

            def take_indices(t, n):
                pool.tensor_copy(so_i[:, :], slots[:, bass.ds(t, 1), 0:2].rearrange("p o f -> p (o f)")).then_inc(idx_taken, 1)
                pool_wait(idx_taken, n)

            def gather_x(w, done):
                pool.indirect_dma_start(out=gath[:, w, :], out_offset=None, in_=x,
                                        in_offset=bass.IndirectOffsetOnAxis(ap=so_i[:, w:w + 1], axis=0)).then_inc(done, 16)

            with pool.Fori(0, tiles) as t:
                pool_wait(l1_slots, t + 1)
                take_indices(t, t + 1)
                gather_x(1, l1_obj)
                gather_x(0, l1_sub)
                pool_wait(l1_tile, t + 2)
            pool.wait_ge(u_stored, 16 * C)
            pool.sem_inc(pool_passed, 1)
            with pool.Fori(0, tiles) as t:
                take_indices(t, tiles + t + 1)
                pool.indirect_dma_start(out=gath_u[:, :], out_offset=None, in_=u_rows,
                                        in_offset=bass.IndirectOffsetOnAxis(ap=so_i[:, 0:1], axis=0)).then_inc(l3_u, 16)
                gather_x(1, l3_obj)
                gather_x(0, l3_sub)
                pool_wait(l3_tile, t + 1)
                pool.dma_start(v_rows[bass.ts(t, P), :], prod).then_inc(v_stored, 16)
                pool_wait(v_stored, t * 16 + 16)
                pool.sem_inc(prod_free, 1)
            pool.wait_ge(bm_stored, 16 * C)
            pool.wait_ge(x1_stored, 16 * C)
            pool.sem_inc(pool_passed, 1)
            with pool.Fori(0, tiles) as t:
                pool_wait(l4_tile, t + 1)
                take_indices(t, tiles * 2 + t + 1)
                pool.indirect_dma_start(out=row_x0, out_offset=None, in_=x1_rows[0:N, :],
                                        in_offset=bass.IndirectOffsetOnAxis(ap=so_i[:, 0:1], axis=0)).then_inc(l4_x0, 16)
                pool.indirect_dma_start(out=bm_e[:, :], out_offset=None, in_=bm_rows,
                                        in_offset=bass.IndirectOffsetOnAxis(ap=so_i[:, 0:1], axis=0)).then_inc(l4_bm, 16)
                with pool.Fori(0, tiles) as o:
                    pool.dma_start(v_other, v_rows[bass.ts(o, P), :]).then_inc(l4_v, 16)
                    pool_wait(l4_sum, t * tiles + o + 1)
                pool_wait(l4_x0, t * 16 + 16)
                pool_wait(l4_x1, t + 1)
                pool.indirect_dma_start(out=x1_rows, out_offset=bass.IndirectOffsetOnAxis(ap=spot_i[:, 0:1], axis=0),
                                        in_=row_x, in_offset=None).then_inc(x1_fixed, 16)
                pool_wait(x1_fixed, t * 16 + 16)
                pool.sem_inc(row_free, 1)

        @block.scalar
        def _(act):
            act.wait_ge(scale_ready, 1)
            for k in range(C):
                act.activation(terms[:, 0, k, :], xs[:, k, :], ACT.Copy, scale=scale[:, 0:1]).then_inc(x_hi, 1)
                if k % 2 == 0:
                    act.wait_ge(stage_in[k % STAGES], 16 * (k // STAGES + 1))
                    rows = P if k < C - 1 else TAIL
                    if k == C - 1:
                        act.wait_ge(pads, 8)
                    act.activation(at[0:rows, k, 0:N], stg[0:rows, k % STAGES, 0:N], ACT.Copy,
                                   accum_out=col_a[0:rows, k:k + 1]).then_inc(at_even, 1)

            def ax_evacuate(i, bank):
                act.wait_ge(ax_done, i + 1)
                act.activation(u[:, i, 0:H], ps[:, bank, :], ACT.Copy, scale=scale[:, 1:2]).then_inc(ax_out, 1)

            def adj_rows(r):
                for n, (lo, hi) in enumerate(PIECES):
                    q = 3 * r + n
                    act.wait_ge(a_piece, q + 1)
                    act.activation(bm[:, r, lo * P:hi * P], ps[:, 6 + q % 2, 0:(hi - lo) * P], ACT.Copy,
                                   accum_out=row3[:, r, n:n + 1]).then_inc(piece_free, 1)

            for i in GROUP_A:
                ax_evacuate(i, i)
            def roots_of(m):
                lo, hi = PARTS[m]
                act.wait_ge(var0, m + 2)
                act.activation(roots[:, :, lo:hi], squares[:, :, lo:hi], ACT.Sqrt).then_inc(std0, 1)

            def dense_norm(m):
                act.wait_ge(nmr_ready, m + 1)
                for i in range(*PARTS[m]):
                    act.activation(xs[:, i, :], xs[:, i, :], ACT.Identity, scale=inverse[:, 0, i:i + 1],
                                   bias=nmr[:, i:i + 1]).then_inc(x1_ready, 1)

            def high_terms(m):
                act.wait_ge(x1_ready, PARTS[m][1])
                for i in range(*PARTS[m]):
                    act.activation(terms[:, 0, i, :], xs[:, i, :], ACT.Copy, scale=dinv_x[:, i:i + 1]).then_inc(xt_hi, 1)

            for m, i in enumerate(GROUP_B[:-1]):
                for r in range(3 * m, min(3 * m + 3, C)):
                    adj_rows(r)
                ax_evacuate(i, i - GROUP_B[0])
                if m == 2:
                    roots_of(0)
            dense_norm(0)
            ax_evacuate(C - 1, GROUP_B[-1] - GROUP_B[0])
            high_terms(0)
            for m in range(1, len(PARTS)):
                roots_of(m)
                dense_norm(m)
                high_terms(m)
            act.activation(warm[:, :], eps_c[:, :], ACT.Exp).then_inc(warmed, 1)
            tiles = loop_tiles(act)
            with act.Fori(0, tiles) as t:
                for w in range(2):
                    act.wait_ge(l1_turned, 2 * t + w + 1)
                    act.activation(gath_t[:, 1 - w, :, :], ps[:, 7 if w else 4, :].rearrange("p (c s) -> p c s", c=HC),
                                   ACT.Copy).then_inc(l1_turned_sb, 1)
                act.wait_ge(l1_k, t + 1)
                act.activation(k_sb, ps[:, 6, :], ACT.Copy).then_inc(l1_k_sb, 1)
            def bx_evacuate(i):
                act.wait_ge(bx_done, i + 1)
                act.activation(u[:, i, 0:H], ps[:, i % 4, :], ACT.Copy).then_inc(bx_out, 1)

            act.wait_ge(u_stored, 16 * C)
            for i in AHEAD:
                bx_evacuate(i)
            with act.Fori(0, tiles) as t:
                act.wait_ge(l2_arg, t + 1)
                act.activation(ex[:, 0:3 * HEADS], ex[:, 0:3 * HEADS], ACT.Exp).then_inc(l2_exp, 1)
            act.activation(warm[:, :], warm[:, :], ACT.Sqrt).then_inc(warmed, 1)
            for i in BESIDE[:-IN_LOOP4]:
                bx_evacuate(i)
            with act.Fori(0, tiles) as t:
                act.wait_ge(l4_var, t + 1)
                act.activation(coef[:, 4:5], coef[:, 3:4], ACT.Sqrt, bias=eps_c[:, 0:1]).then_inc(l4_root, 1)
                with act.If(t < 1):
                    for i in BESIDE[-IN_LOOP4:]:
                        bx_evacuate(i)
            for i in range(C):
                act.wait_ge(last_added, i + 1)
                act.activation(terms[:, 0, i, :], u[:, i, 0:H], ACT.Copy, scale=dinv_z[:, i:i + 1]).then_inc(zt_hi, 1)
            for i in range(C):
                act.wait_ge(var1, i + 1)
                act.activation(std[:, i:i + 1], mv[:, i, 1:2], ACT.Sqrt, bias=eps_c[:, 0:1]).then_inc(std1, 1)

        @block.tensor
        def _(pe):
            def together_step(k, first, last, bank_free, ready, matrix, done, chunks=GROUP_A):
                ready(k)
                for i in chunks:
                    if first:
                        bank_free(i)
                    for s in range(2):
                        m = pe.matmul(ps[:, i, :], matrix[:, k, i * P:(i + 1) * P], terms[:, s, k, :],
                                      start=first and s == 0, stop=last and s == 1)
                    if last:
                        m.then_inc(done, 1)

            def in_turn(first, last, bank_free, bank_of, matrix, done, beside=None):
                def one_chunk(i):
                    bank_free(i)
                    for k in range(C):
                        for s in range(2):
                            m = pe.matmul(ps[:, bass.ds(bank_of(i), 1), :].rearrange("p o d -> p (o d)"),
                                          matrix[:, k, bass.ts(i, P)], terms[:, s, k, :],
                                          start=(k == 0 and s == 0), stop=(k == C - 1 and s == 1))
                        if beside and k < C - 1:
                            beside(i, k)
                    m.then_inc(done, 1)

                if last - first == 1:
                    one_chunk(first)
                else:
                    with pe.Fori(first, last) as i:
                        one_chunk(i)

            pe.wait_ge(consts, 6)
            pe.wait_ge(peak_found, 1)
            pe.transpose(ps[0:1, 7, 0:P], peak[:, 0:1], ident[:, :]).then_inc(peak_row, 1)
            pe.wait_ge(pads, 8)
            pe.wait_ge(scale_found, 1)
            pe.matmul(ps[:, 7, P:P + 2], ones[0:1, :], peak_i[0:1, 2:4].bitcast(f32), start=True, stop=True).then_inc(scale_row, 1)

            for k in range(C):
                pe.wait_ge(at_odd if k % 2 else at_even, k // 2 + 1)
                together_step(k, k == 0, k == C - 1, lambda i: None, lambda k: pe.wait_ge(x_lo, k + 1), at, ax_done)

            def adj_piece(i, k):
                m, a, n = i - GROUP_B[0], k // 3, k % 3
                if k >= 3 * min(3, C - 3 * m if isinstance(m, int) else 3):
                    return
                lo, hi = PIECES[n]
                pe.wait_ge(piece_free, 9 * m + 3 * a + n + 1)
                for j in range(lo, hi):
                    piece = pe.matmul(ps[:, bass.ds((i + a + n) % 2 + 6, 1), (j - lo) * P:(j - lo + 1) * P].rearrange("p o d -> p (o d)"),
                                      at[:, j, bass.ts(3 * m + a, P)], ident16[:, :], start=True, stop=True)
                piece.then_inc(a_piece, 1)

            def ax_bank(i):
                return i - GROUP_B[0]

            def ax_free(i):
                pe.wait_ge(ax_out, ax_bank(i) + 1)

            in_turn(GROUP_B[0], C - 2, ax_free, ax_bank, at, ax_done, beside=adj_piece)
            in_turn(C - 2, C - 1, ax_free, ax_bank, at, ax_done, beside=adj_piece)
            in_turn(C - 1, C, ax_free, ax_bank, at, ax_done)

            pe.wait_ge(ax_out, C)

            def bx_step(k):
                together_step(k, k == 0, k == C - 1, lambda i: None, lambda k: pe.wait_ge(xt_lo, k + 1), bm, bx_done, AHEAD)

            def bx_chunks(first, n):
                for i in BESIDE[first:first + n]:
                    in_turn(i, i + 1, lambda i: pe.wait_ge(bx_out, i - 3), lambda i: i % 4, bm, bx_done)

            for k in range(0, 5):
                bx_step(k)
            pe.wait_ge(base_in, 1)
            pe.matmul(ps[:, 5, 0:1], above16[:, :], total16[:, :], start=True, stop=True)
            pe.matmul(ps[:, 5, 1:2], ones16[:, :], total16[:, :], start=True, stop=True).then_inc(base_done, 1)

            bx_step(5)
            tiles = loop_tiles(pe)
            with pe.Fori(0, tiles) as t:
                for c in range(EC):
                    if c % BLOCK == 0:
                        pe.wait_ge(l1_onehot, t * (ECP // BLOCK) + c // BLOCK + 1)
                    m = pe.matmul(ps[:, 7, 0:3], onehot[:, c // BLOCK, :, c % BLOCK], code[:, c, :], start=(c == 0), stop=(c == EC - 1))
                m.then_inc(l1_packed, 1)
            pe.wait_ge(w_in, 32)
            pe.wait_ge(bias_in, 32)
            bx_step(6)
            bx_step(7)
            with pe.Fori(0, tiles) as t:
                pe.wait_ge(l1_tile, t + 1)
                for w, got in ((1, l1_obj), (0, l1_sub)):
                    pe.wait_ge(got, 16 * t + 16)
                    for c in range(HC):
                        m = pe.transpose(ps[:, 4 if w else 7, c * P:(c + 1) * P], gath[:, w, c * P:(c + 1) * P], ident[:, :])
                    m.then_inc(l1_turned, 1)
                for n, (w, done) in enumerate(((1, l1_k), (0, l1_q))):
                    pe.matmul(ps[:, 5 + w, :], ones[0:1, :], biases[0:1, w, :], start=True, stop=False)
                    pe.wait_ge(l1_turned_sb, 2 * t + 1 + n)
                    for c in range(HC):
                        m = pe.matmul(ps[:, 5 + w, :], gath_t[:, w, c, :], w_sb[:, w, c, :], start=False, stop=(c == HC - 1))
                    m.then_inc(done, 1)
            for k in range(8, C):
                bx_step(k)
            with pe.Fori(0, tiles) as t:
                with pe.Fori(0, tiles) as o:
                    pe.wait_ge(id_diag, t * tiles + o + 1)
                    pe.matmul(ps[:, 7, 0:2 * P], ones[:, :], words[:, 8 * P:10 * P], start=True, stop=True).then_inc(id_row, 1)
                    pe.wait_ge(s_diag, t * tiles + o + 1)
                    for g in range(2):
                        m = pe.matmul(ps[:, 4 + g, :], ones[:, :], words[:, g * 512:(g + 1) * 512], start=True, stop=True)
                    m.then_inc(s_row, 1)

                with pe.If(t < 1):
                    bx_chunks(0, IN_LOOP2)

            with pe.Fori(0, tiles) as t:
                pe.wait_ge(l3_diag, t + 1)
                pe.matmul(ps[:, 7, 0:P], ones[:, :], diag[:, 8, :], start=True, stop=True).then_inc(l3_row, 1)
                with pe.Fori(0, tiles) as o:
                    pe.wait_ge(l3_same, t * tiles + o + 1)
                    pe.matmul(ps[:, 6, 0:EX_N], same[:, :], ex_other[:, :], start=True, stop=True).then_inc(l3_sum, 1)
                with pe.If(t < 1):
                    bx_chunks(IN_LOOP2, IN_LOOP3)
            bx_chunks(IN_LOOP2 + IN_LOOP3, len(BESIDE) - IN_LOOP2 - IN_LOOP3 - IN_LOOP4)

            def change_product(c, done, added, before):
                if c >= 2:
                    pe.wait_ge(added, before + c - 1)
                for s in range(2):
                    m = pe.matmul(ps[:, 6 + c % 2, :], bm_e[:, c * P:(c + 1) * P], dz[:, s, :], start=(s == 0), stop=(s == 1))
                m.then_inc(done, 1)

            with pe.Fori(0, tiles) as t:
                with pe.If(t > 0):
                    pe.wait_ge(l4_dz, t + 1)
                    for c in range(C):
                        change_product(c, l4_done, l4_added, t * C)
                pe.wait_ge(l4_diag, t + 1)
                pe.matmul(ps[:, 7, 0:P], ones[:, :], diag[:, 8, :], start=True, stop=True).then_inc(l4_row, 1)
                with pe.Fori(0, tiles) as o:
                    pe.wait_ge(l4_v, (t * tiles + o) * 16 + 16)
                    pe.wait_ge(l4_same, t * tiles + o + 1)
                    pe.matmul(ps[:, 6, :], same[:, :], v_other, start=True, stop=True).then_inc(l4_sum, 1)
                with pe.If(t < 1):
                    bx_chunks(len(BESIDE) - IN_LOOP4, IN_LOOP4)
            pe.wait_ge(l4_dz, tiles + 1)
            change_product(0, last_done, last_added, 0)
            change_product(1, last_done, last_added, 0)
            pe.wait_ge(bx_out, C)
            for k in range(C):
                if k + 2 < C:
                    change_product(k + 2, last_done, last_added, 0)
                together_step(k, k == 0, k == C - 1, lambda i: None, lambda k: pe.wait_ge(zt_lo, k + 1), at, y_done)
            pe.wait_ge(last_added, C)
            in_turn(6, 8, lambda i: None, lambda i: i, at, y_done)
            in_turn(8, C, lambda i: pe.wait_ge(y_added, i - 7), lambda i: i - 8, at, y_done)

        @block.vector
        def _(dve):
            main = Steps(dve, v_step)
            dve.memset(raw[:, :, :], N).then_inc(pads, 1)
            dve.memset(xs[:, C - 1, :], 0.0).then_inc(pads, 1)
            dve.memset(a_ii[:, :], 0.0).then_inc(pads, 1)
            dve.memset(col_a[:, C - 1:C], 0.0).then_inc(pads, 1)
            dve.memset(eps_c[:, :], EPS).then_inc(pads, 1)
            dve.memset(at[:, C - 1, :], 0.0).then_inc(pads, 1)
            dve.memset(at[:, 0:C - 1, N:NP], 0.0).then_inc(pads, 1)
            dve.memset(ones[:, :], 1.0).then_inc(pads, 1)
            dve.sem_inc(piece_free, 2)
            dve.sem_inc(prod_free, 1)
            dve.sem_inc(row_free, 1)
            dve.sem_inc(l1_tile, 1)
            dve.sem_inc(l4_dz, 1)
            dve.sem_inc(l4_done, C)
            dve.sem_inc(l4_added, C)
            main(dve.memset(ones16[:, :], 1.0))
            main(dve.memset(onecol[:, :], 1.0))
            main(dve.memset(rank16[:, :], 0.0))
            dve.wait_ge(pairs_in, 32)
            main(dve.tensor_copy(pf[:, :, :], raw[:, :, :]))
            main(dve.tensor_scalar(pg[:, :, :], pf[:, :, :], 0.0, float(N), ALU.is_lt, ALU.mult))
            main(dve.tensor_tensor(pf[:, :, :], pf[:, :, :], pg[:, :, :], ALU.add))
            main(dve.tensor_scalar(pg[:, :, :], pf[:, :, :], 0.0, None, ALU.is_ge))
            main(dve.scalar_tensor_tensor(pg[:, :, :], pf[:, :, :], float(N), pg[:, :, :], ALU.is_lt, ALU.mult))
            main(dve.tensor_tensor(ok[:, :], pg[:, :, 0], pg[:, :, 1], ALU.mult))
            main(dve.tensor_tensor(ok2[:, :], pf[:, :, 0], pf[:, :, 1], ALU.not_equal))
            main(dve.tensor_tensor(ok[:, :], ok[:, :], ok2[:, :], ALU.mult))
            main(dve.scalar_tensor_tensor(ok2[:, :], pf[:, :, 1], float(N), pf[:, :, 0], ALU.mult, ALU.add))
            dve.tensor_tensor(at_idx[:, :], ok2[:, :], ok[:, :], ALU.mult).then_inc(idx_ready, 1)
            main(dve.tensor_tensor(code[:, :, 0], pf[:, :, 0], ok[:, :], ALU.mult))
            main(dve.tensor_tensor(code[:, :, 1], pf[:, :, 1], ok[:, :], ALU.mult))
            main(dve.tensor_copy(code[:, :, 2], ok[:, :]))
            dve.wait_ge(x_in[0], 16)
            dve.tensor_reduce(peak[:, 1:2], xs[:, 0:HALF, :].rearrange("p c d -> p (c d)"), AX.X, ALU.max,
                              apply_absolute_value=True).then_inc(v_step, 1)
            dve.wait_ge(x_in[1], 32)
            dve.tensor_reduce(peak[:, 2:3], xs[:, HALF:C, :].rearrange("p c d -> p (c d)"), AX.X, ALU.max,
                              apply_absolute_value=True).then_inc(v_step, 1)
            main.n += 2
            dve.wait_ge(v_step, main.n)
            dve.tensor_tensor(peak[:, 0:1], peak[:, 1:2], peak[:, 2:3], ALU.max).then_inc(peak_found, 1)
            dve.wait_ge(peak_row, 1)
            main(dve.tensor_reduce(peak[0:1, 3:4], ps[0:1, 7, 0:P], AX.X, ALU.max))
            main(dve.tensor_scalar(peak_i[:, 0:1], peak[0:1, 3:4].bitcast(i32), EXPONENT, None, ALU.bitwise_and))
            main(dve.tensor_scalar(peak_i[:, 1:2], peak_i[:, 0:1], float(32 << 23), None, ALU.max))
            main(dve.tensor_scalar(peak_i[:, 2:3], peak_i[:, 1:2], -1.0, float(TOP << 23), ALU.mult, ALU.add))
            dve.tensor_scalar(peak_i[:, 3:4], peak_i[:, 1:2], float((254 - TOP) * (1 << 23)), None, ALU.add).then_inc(scale_found, 1)
            dve.wait_ge(scale_row, 1)
            dve.tensor_copy(scale[:, :], ps[:, 7, P:P + 2]).then_inc(scale_ready, 1)
            dve.wait_ge(scale_ready, 1)
            for k in range(C):
                if k % 2:
                    dve.wait_ge(stage_in[k % STAGES], 16 * (k // STAGES + 1))
                    dve.tensor_scalar(at[:, k, 0:N], stg[:, k % STAGES, 0:N], 1.0, 0.0, ALU.mult, ALU.add,
                                      accum_out=col_a[:, k:k + 1]).then_inc(at_odd, 1)
                dve.wait_ge(x_hi, k + 1)
                dve.scalar_tensor_tensor(terms[:, 1, k, :], xs[:, k, :], scale[:, 0:1], terms[:, 0, k, :],
                                         ALU.mult, ALU.subtract).then_inc(x_lo, 1)
            dve.wait_ge(consts, 6)
            main(dve.tensor_copy(slot_cols[:, :, :], slot_row[:, :].rearrange("p (s o) -> p s o", o=1).to_broadcast([P, P, BLOCK])))
            dve.wait_ge(aii_in, 32)

            def dense_finish(m):
                lo, hi = PARTS[m]
                dve.wait_ge(std0, m + 1)
                main(dve.reciprocal(inverse[:, :, lo:hi], roots[:, :, lo:hi]))
                dve.tensor_scalar(dinv_x[:, lo:hi], inverse[:, 1, lo:hi], XS, None, ALU.mult).then_inc(v_step, 1)
                dve.tensor_scalar(dinv_z[:, lo:hi], inverse[:, 1, lo:hi], 0.5 * ZS / XS, None, ALU.mult).then_inc(v_step, 1)
                dve.scalar_tensor_tensor(nmr[:, lo:hi], mv[:, lo:hi, 0], -1.0, inverse[:, 0, lo:hi], ALU.mult, ALU.mult).then_inc(v_step, 1)
                dve.tensor_scalar(u[:, lo:hi, H + 2], inverse[:, 1, lo:hi], XS, None, ALU.mult).then_inc(v_step, 1)
                main.n += 4
                dve.wait_ge(v_step, main.n)
                dve.sem_inc(nmr_ready, 1)
                dve.sem_inc(counts_ready, 1)

            def low_term(i):
                dve.wait_ge(xt_hi, i + 1)
                dve.scalar_tensor_tensor(terms[:, 1, i, :], xs[:, i, :], dinv_x[:, i:i + 1], terms[:, 0, i, :],
                                         ALU.mult, ALU.subtract).then_inc(xt_lo, 1)

            def two_way(m):
                for r in range(*BATCHES[m]):
                    dve.wait_ge(piece_free, 3 * r + 5)
                    main(dve.tensor_tensor(bm[:, r, :], bm[:, r, :], at[:, r, :], ALU.add))
                    dve.scalar_tensor_tensor(bm[:, r, r * P:(r + 1) * P], ident16[:, :], 2.0, bm[:, r, r * P:(r + 1) * P],
                                             ALU.mult, ALU.add).then_inc(bm_row, 1)

            def dense_rows(m):
                lo, hi = BATCHES[m]
                main(dve.tensor_reduce(row_a[:, lo:hi], row3[:, lo:hi, :], AX.X, ALU.add))
                dve.tensor_tensor(col_a[:, lo:hi], col_a[:, lo:hi], row_a[:, lo:hi], ALU.add).then_inc(v_step, 1)
                main.n += 1
                main(dve.tensor_tensor(row_a[:, lo:hi], row_a[:, lo:hi], a_ii[:, lo:hi], ALU.subtract))
                dve.tensor_copy(u[:, lo:hi, H], row_a[:, lo:hi]).then_inc(v_step, 1)
                dve.tensor_copy(u[:, lo:hi, H + 1], a_ii[:, lo:hi]).then_inc(v_step, 1)
                dve.tensor_scalar(squares[:, 1, lo:hi], col_a[:, lo:hi], 0.5, 1.0, ALU.mult, ALU.add).then_inc(v_step, 1)
                main.n += 3
                main(dve.tensor_scalar(one_z[:, lo:hi], row_a[:, lo:hi], E_ZERO, 1.0, ALU.mult, ALU.add))
                main(dve.tensor_scalar(ratio[:, lo:hi], one_z[:, lo:hi], 1.0, 1.0 / E_ZERO, ALU.add, ALU.mult))
                main(dve.tensor_tensor(ratio[:, lo:hi], ratio[:, lo:hi], a_ii[:, lo:hi], ALU.subtract))
                dve.wait_ge(x_lo, C)
                for i in range(lo, hi):
                    dve.wait_ge(ax_out, i + 1)
                    dve.scalar_tensor_tensor(xs[:, i, :], xs[:, i, :], ratio[:, i:i + 1], u[:, i, 0:H], ALU.mult, ALU.add).then_inc(v_step, 1)
                main.n += hi - lo
                for i in range(lo, hi):
                    dve.wait_ge(v_step, main.n)
                    dve.bn_stats(stats[:, i, :], xs[:, i, :]).then_inc(v_step, 1)
                main.n += hi - lo
                for i in range(lo, hi):
                    dve.wait_ge(v_step, main.n)
                    dve.bn_aggr(mv[:, i, :], stats[:, i, :]).then_inc(v_step, 1)
                main.n += hi - lo
                main(dve.tensor_scalar(one_z[:, lo:hi], one_z[:, lo:hi], EPS ** 0.5 / E_ZERO, None, ALU.mult))
                main(dve.tensor_tensor(one_z[:, lo:hi], one_z[:, lo:hi], one_z[:, lo:hi], ALU.mult))
                dve.tensor_tensor(squares[:, 0, lo:hi], mv[:, lo:hi, 1], one_z[:, lo:hi], ALU.add).then_inc(var0, 1)

            def low_terms(first, last):
                for i in range(first, last):
                    low_term(i)

            two_way(0)
            dense_rows(0)
            two_way(1)
            dense_rows(1)
            two_way(2)
            dense_finish(0)
            dense_rows(2)
            low_terms(0, 2)
            two_way(3)
            dense_finish(1)
            low_terms(2, 5)
            dense_rows(3)
            dve.wait_ge(kept_in, 16 * EC)
            main(dve.scalar_tensor_tensor(ok[:, :], kept[:, :], 1.0, ok[:, :], ALU.is_equal, ALU.mult))
            main(dve.tensor_tensor_scan(rank[:, :], onecol[:, :], ok[:, :], 0.0, ALU.mult, ALU.add))
            dve.tensor_copy(total16[:, :], rank[:, EC - 1:EC]).then_inc(base_in, 1)
            dve.wait_ge(base_done, 1)
            main(dve.tensor_copy(base[:, :], ps[:, 5, 0:2]))
            main(dve.scalar_tensor_tensor(rank[:, :], rank[:, :], base[:, 0:1], ok[:, :], ALU.add, ALU.mult))
            main(dve.tensor_scalar(count_i[:, 0:1], base[:, 1:2], 1.0, float(P - 1), ALU.max, ALU.add))
            dve.tensor_scalar(tiles_i[:, :], count_i[:, 0:1], 7, None, ALU.logical_shift_right).then_inc(tiles_ready, 1)
            dense_finish(2)
            low_terms(5, 6)
            tiles = loop_tiles(dve)

            def held(t, table):
                return table[:, bass.ds(t, 1), :].rearrange("p o f -> p (o f)")

            def spread(columns, n):
                return columns.rearrange("p (h o) -> p h o", o=1).to_broadcast([P, n, P])

            def eyes(n):
                return ident[:, :].rearrange("p (o s) -> p o s", o=1).to_broadcast([P, n, P])

            with dve.Fori(0, tiles) as t:
                step = Steps(dve, l1_step, t * PACK_STEPS)
                step(dve.tensor_copy(rank16[:, 0:EC], rank[:, :]))
                for b in range(ECP // BLOCK):
                    dve.tensor_tensor(onehot[:, b, :, :],
                                      rank16[:, b * BLOCK:(b + 1) * BLOCK].rearrange("p (o c) -> p o c", o=1).to_broadcast([P, P, BLOCK]),
                                      slot_cols[:, :, :], ALU.is_equal).then_inc(l1_onehot, 1)
                dve.wait_ge(l1_packed, t + 1)
                step(dve.tensor_copy(so[:, 0:3], ps[:, 7, 0:3]))
                dve.scalar_tensor_tensor(so[:, KEY:KEY + 1], so[:, SUB:SUB + 1], float(N), so[:, OBJ:OBJ + 1],
                                         ALU.mult, ALU.add).then_inc(l1_step, 1)
                step.n += 1
                step(dve.tensor_scalar(so[:, SUB1:SUB1 + 1], so[:, SUB:SUB + 1], so[:, USED:USED + 1], -1.0, ALU.add, ALU.add))
                dve.tensor_copy(held(t, slots), so[:, :]).then_inc(l1_slots, 1)
                step(dve.tensor_scalar(rank[:, :], rank[:, :], -float(P), None, ALU.add))
                assert step.n == PACK_STEPS, step.n
                dve.wait_ge(l1_slots, t + 1)

            low_terms(6, C)
            with dve.Fori(0, tiles) as t:
                step = Steps(dve, score_step, t * SCORE_STEPS)
                step(dve.tensor_copy(so[:, :], held(t, slots)))
                dve.wait_ge(l1_q, t + 1)
                dve.wait_ge(l1_k_sb, t + 1)
                step(dve.tensor_tensor(prod, ps[:, 5, :], k_sb, ALU.mult))
                step(dve.tensor_reduce(s8[:, :], prod.rearrange("p (h d) -> p h d", h=HEADS), AX.X, ALU.add))
                dve.tensor_scalar(held(t, scores), s8[:, :], 1.0 / float(DK) ** 0.5, so[:, USED:USED + 1],
                                  ALU.mult, ALU.mult).then_inc(l1_tile, 1)
                assert step.n == SCORE_STEPS, step.n
                dve.wait_ge(l1_tile, t + 2)

            with dve.Fori(0, tiles) as t:
                step = Steps(dve, l2_step, t * LOOP2_STEPS)
                dve.tensor_copy(so[:, :], held(t, slots)).then_inc(l2_step, 1)
                dve.tensor_copy(s8[:, :], held(t, scores)).then_inc(l2_step, 1)
                dve.memset(m8[:, :], DIAG).then_inc(l2_step, 1)
                dve.memset(earlier[:, :], 0.0).then_inc(l2_step, 1)
                step.n = 4
                step(dve.tensor_copy(ahead[:, :], slot_id[:, bass.ds(t, 1)]))
                dve.sem_inc(v_passed, 1)
                with dve.Fori(0, tiles) as o:
                    turn = t * tiles + o
                    one = Steps(dve, row_step, turn * ROW_STEPS)
                    dve.tensor_copy(s_other[:, :], held(o, scores)).then_inc(row_step, 1)
                    one.n += 1
                    one(dve.tensor_copy(other[:, :], held(o, slots)[:, SUB1:KEY + 1]))
                    dve.tensor_tensor(diag[:, 8:10, :], eyes(2), spread(other[:, :], 2), ALU.mult).then_inc(id_diag, 1)
                    dve.tensor_tensor(diag[:, 0:HEADS, :], eyes(HEADS), spread(s_other[:, :], HEADS), ALU.mult).then_inc(s_diag, 1)
                    dve.wait_ge(id_row, turn + 1)
                    dve.tensor_scalar(same_row[:, :], ps[:, 7, 0:P], so[:, SUB1:SUB1 + 1], None, ALU.is_equal).then_inc(row_step, 1)
                    one.n += 1
                    one(dve.tensor_scalar(same_key[:, :], ps[:, 7, P:2 * P], so[:, KEY:KEY + 1], None, ALU.is_equal))
                    dve.tensor_scalar(same[:, :], same_row[:, :], -1.0, FAR, ALU.add, ALU.mult).then_inc(row_step, 1)
                    dve.wait_ge(row_step, one.base + one.n)
                    one.n += 1
                    dve.scalar_tensor_tensor(same_row[:, :], slot_col[:, :], ahead[:, :], same_row[:, :], ALU.is_lt, ALU.mult,
                                             accum_out=earlier[:, 2:3]).then_inc(row_step, 1)
                    one.n += 1
                    one(dve.scalar_tensor_tensor(same_key[:, :], slot_col[:, :], ahead[:, :], same_key[:, :], ALU.is_lt, ALU.mult,
                                                 accum_out=earlier[:, 3:4]))
                    dve.tensor_tensor(earlier[:, 0:2], earlier[:, 0:2], earlier[:, 2:4], ALU.add).then_inc(row_step, 1)
                    one.n += 1
                    one(dve.tensor_scalar(ahead[:, :], ahead[:, :], -float(P), None, ALU.add))
                    dve.wait_ge(s_row, turn + 1)
                    one(dve.tensor_tensor(far, ps[:, 4:6, :].rearrange("p b (h s) -> p (b h) s", s=P),
                                          same[:, :].rearrange("p (o s) -> p o s", o=1).to_broadcast([P, HEADS, P]), ALU.add))
                    one(dve.tensor_reduce(m_new[:, :], far, AX.X, ALU.max))
                    one(dve.tensor_tensor(m8[:, :], m8[:, :], m_new[:, :], ALU.max))
                    assert one.n == ROW_STEPS, one.n
                dve.tensor_tensor(ex[:, EX_S:EX_S + HEADS], s8[:, :], m8[:, :], ALU.subtract).then_inc(l2_step, 1)
                dve.tensor_scalar(ex[:, EX_0:EX_0 + HEADS], m8[:, :], -1.0, None, ALU.mult).then_inc(l2_step, 1)
                step.n += 2
                step(dve.tensor_scalar(ex[:, EX_D:EX_D + HEADS], m8[:, :], -1.0, DIAG, ALU.mult, ALU.add))
                dve.sem_inc(l2_arg, 1)
                step(dve.tensor_scalar(ex[:, EX_ONE:EX_ONE + 1], earlier[:, 1:2], 0.0, so[:, USED:USED + 1], ALU.is_equal, ALU.mult))
                step(dve.tensor_scalar(ex[:, EX_FIRST:EX_FIRST + 1], earlier[:, 0:1], 0.0, so[:, USED:USED + 1], ALU.is_equal, ALU.mult))
                dve.wait_ge(l2_exp, t + 1)
                step(dve.tensor_scalar(ex[:, EX_S:EX_S + HEADS], ex[:, EX_S:EX_S + HEADS], ex[:, EX_ONE:EX_ONE + 1], None, ALU.mult))
                step(dve.tensor_copy(held(t, exps), ex[:, :]))
                assert step.n == LOOP2_STEPS, step.n

            with dve.Fori(0, tiles) as t:
                step = Steps(dve, l3_step, t * LOOP3_STEPS)
                step(dve.tensor_copy(so[:, :], held(t, slots)))
                dve.tensor_scalar(diag[:, 8, :], ident[:, :], so[:, SUB1:SUB1 + 1], None, ALU.mult).then_inc(l3_diag, 1)
                dve.memset(z_sum[:, :], 0.0).then_inc(l3_step, 1)
                step.n += 1
                step(dve.tensor_copy(ex[:, :], held(t, exps)))
                dve.wait_ge(l3_row, t + 1)
                dve.sem_inc(v_passed, 1)
                with dve.Fori(0, tiles) as o:
                    turn = t * tiles + o
                    one = Steps(dve, sum_step, turn * SUM_STEPS)
                    dve.tensor_copy(ex_other[:, :], held(o, exps)).then_inc(sum_step, 1)
                    one.n += 1
                    one(dve.tensor_copy(other[:, 0:1], held(o, slots)[:, SUB1:SUB1 + 1]))
                    dve.tensor_scalar(same[:, :], ps[:, 7, 0:P], other[:, 0:1], None, ALU.is_equal).then_inc(l3_same, 1)
                    dve.wait_ge(l3_sum, turn + 1)
                    one(dve.tensor_tensor(z_sum[:, :], z_sum[:, :], ps[:, 6, 0:EX_N], ALU.add))
                    assert one.n == SUM_STEPS, one.n
                dve.wait_ge(l3_u, 16 * t + 16)
                step(dve.tensor_scalar(coef[:, 0:1], gath_u[:, H:H + 1], z_sum[:, EX_ONE:EX_ONE + 1], None, ALU.subtract))
                step(dve.scalar_tensor_tensor(zz[:, :], ex[:, EX_0:EX_0 + HEADS], coef[:, 0:1], ex[:, EX_D:EX_D + HEADS], ALU.mult, ALU.add))
                step(dve.tensor_tensor(zz[:, :], zz[:, :], z_sum[:, EX_S:EX_S + HEADS], ALU.add))
                step(dve.reciprocal(zz[:, :], zz[:, :]))
                step(dve.tensor_tensor(shares[:, :, :], ex[:, 0:3 * HEADS].rearrange("p (a h) -> p a h", a=3),
                                       zz[:, :].rearrange("p (o h) -> p o h", o=1).to_broadcast([P, 3, HEADS]), ALU.mult))
                step(dve.tensor_reduce(wcd[:, :], shares[:, :, :], AX.X, ALU.add))
                step(dve.tensor_scalar(wcd[:, :], wcd[:, :], 1.0 / HEADS, None, ALU.mult))
                dve.scalar_tensor_tensor(coef[:, 1:2], wcd[:, 1:2], ex[:, EX_ONE:EX_ONE + 1], wcd[:, 0:1], ALU.mult, ALU.subtract).then_inc(l3_step, 1)
                dve.tensor_tensor(coef[:, 2:3], wcd[:, 1:2], ex[:, EX_FIRST:EX_FIRST + 1], ALU.mult).then_inc(l3_step, 1)
                dve.tensor_tensor(held(t, change), gath_u[:, H + 2:H + 3], ex[:, EX_FIRST:EX_FIRST + 1], ALU.mult).then_inc(l3_step, 1)
                step.n += 3
                step(dve.tensor_scalar(coef[:, 3:4], wcd[:, 2:3], 1.0, ex[:, EX_FIRST:EX_FIRST + 1], ALU.add, ALU.mult))
                step(dve.scalar_tensor_tensor(coef[:, 3:4], coef[:, 2:3], gath_u[:, H + 1:H + 2], coef[:, 3:4], ALU.mult, ALU.subtract))
                dve.wait_ge(prod_free, t + 1)
                dve.wait_ge(l3_obj, 16 * t + 16)
                step(dve.tensor_scalar(prod, gath[:, 1, :], coef[:, 1:2], None, ALU.mult))
                step(dve.scalar_tensor_tensor(prod, gath_u[:, 0:H], coef[:, 2:3], prod, ALU.mult, ALU.subtract))
                dve.wait_ge(l3_sub, 16 * t + 16)
                dve.scalar_tensor_tensor(prod, gath[:, 0, :], coef[:, 3:4], prod, ALU.mult, ALU.subtract).then_inc(l3_tile, 1)
                assert step.n == LOOP3_STEPS, step.n

            with dve.Fori(0, tiles) as t:
                with dve.If(t > 0):
                    dve.wait_ge(bx_out, C)
                    for c in range(C):
                        dve.wait_ge(l4_done, C * t + c + 1)
                        dve.tensor_tensor(u[:, c, 0:H], u[:, c, 0:H], ps[:, 6 + c % 2, :], ALU.add).then_inc(l4_added, 1)
                    dve.wait_ge(l4_added, C * t + C)
                    dve.sem_inc(v_passed, 1)
                dve.sem_inc(l4_tile, 1)
                step = Steps(dve, l4_step, t * LOOP4_STEPS)
                step(dve.tensor_copy(so[:, :], held(t, slots)))
                dve.tensor_scalar(diag[:, 8, :], ident[:, :], so[:, SUB1:SUB1 + 1], None, ALU.mult).then_inc(l4_diag, 1)
                dve.wait_ge(row_free, t + 1)
                dve.memset(row_x, 0.0).then_inc(l4_step, 1)
                dve.tensor_copy(ex[:, EX_FIRST:EX_FIRST + 1], held(t, exps)[:, EX_FIRST:EX_FIRST + 1]).then_inc(l4_step, 1)
                dve.tensor_copy(coef[:, 0:1], held(t, change)).then_inc(l4_step, 1)
                step.n += 3
                step(dve.tensor_scalar(spot[:, 0:1], slot_id[:, 0:1], float(N), None, ALU.add))
                step(dve.tensor_tensor(spot[:, 1:2], so[:, SUB:SUB + 1], spot[:, 0:1], ALU.subtract))
                step(dve.scalar_tensor_tensor(spot[:, 2:3], spot[:, 1:2], ex[:, EX_FIRST:EX_FIRST + 1], spot[:, 0:1], ALU.mult, ALU.add))
                step(dve.tensor_copy(spot_i[:, :], spot[:, 2:3]))
                dve.wait_ge(l4_row, t + 1)
                dve.sem_inc(v_passed, 1)
                with dve.Fori(0, tiles) as o:
                    turn = t * tiles + o
                    one = Steps(dve, total_step, turn * TOTAL_STEPS)
                    one(dve.tensor_copy(other[:, 0:1], held(o, slots)[:, SUB1:SUB1 + 1]))
                    dve.tensor_scalar(same[:, :], ps[:, 7, 0:P], other[:, 0:1], None, ALU.is_equal).then_inc(l4_same, 1)
                    dve.wait_ge(l4_sum, turn + 1)
                    one(dve.tensor_tensor(row_x, row_x, ps[:, 6, :], ALU.subtract))
                    assert one.n == TOTAL_STEPS, one.n
                dve.sem_inc(v_passed, 1)
                step(dve.bn_stats(stats[:, 0, :], row_x))
                dve.sem_inc(v_passed, 1)
                step(dve.bn_aggr(coef[:, 2:4], stats[:, 0, :]))
                dve.sem_inc(l4_var, 1)
                dve.wait_ge(l4_root, t + 1)
                step(dve.reciprocal(coef[:, 1:2], coef[:, 4:5]))
                step(dve.tensor_scalar(row_x, row_x, coef[:, 2:3], coef[:, 1:2], ALU.subtract, ALU.mult))
                dve.sem_inc(l4_x1, 1)
                dve.wait_ge(l4_x0, t * 16 + 16)
                step(dve.tensor_tensor(row_x0, row_x, row_x0, ALU.subtract))
                step(dve.tensor_scalar(dz[:, 0, :], row_x0, coef[:, 0:1], None, ALU.mult))
                step(dve.scalar_tensor_tensor(dz[:, 1, :], row_x0, coef[:, 0:1], dz[:, 0, :], ALU.mult, ALU.subtract))
                dve.wait_ge(l4_bm, t * 16 + 16)
                dve.sem_inc(l4_dz, 1)
                assert step.n == LOOP4_STEPS, step.n

            for i in range(C + 1):
                if i < C:
                    dve.wait_ge(last_done, i + 1)
                    if i == 0:
                        dve.wait_ge(bx_out, C)
                    dve.tensor_tensor(u[:, i, 0:H], u[:, i, 0:H], ps[:, 6 + i % 2, :], ALU.add).then_inc(last_added, 1)
                if i:
                    dve.wait_ge(zt_hi, i)
                    dve.scalar_tensor_tensor(terms[:, 1, i - 1, :], u[:, i - 1, 0:H], dinv_z[:, i - 1:i], terms[:, 0, i - 1, :],
                                             ALU.mult, ALU.subtract).then_inc(zt_lo, 1)
            dve.wait_ge(x1_in, 16 * C)
            for i in range(C):
                dve.wait_ge(y_done, i + 1)
                dve.scalar_tensor_tensor(xs[:, i, :], ps[:, i % 8, :], 1.0 / ZS, xs[:, i, :],
                                         ALU.mult, ALU.add).then_inc(y_added, 1)
                dve.wait_ge(y_added, i + 1)
                main(dve.bn_stats(stats[:, i, :], xs[:, i, :]))
                dve.bn_aggr(mv[:, i, :], stats[:, i, :]).then_inc(var1, 1)
                dve.wait_ge(std1, i + 1)
                main(dve.reciprocal(rstd[:, i:i + 1], std[:, i:i + 1]))
                dve.tensor_scalar(xs[:, i, :], xs[:, i, :], mv[:, i, 0:1], rstd[:, i:i + 1],
                                  ALU.subtract, ALU.mult).then_inc(scaled, 1)


def kernel(x, adj, L0_gnn_rel_pair_index, L0_gnn_Wq, L0_gnn_bq, L0_gnn_Wk, L0_gnn_bk):
    import numpy as np
    import concourse.bacc as bacc
    from concourse.bass_utils import run_bass_kernel_spmd

    laid_out = {
        "x": np.ascontiguousarray(x),
        "adj_t": np.ascontiguousarray(np.asarray(adj).T),
        "pairs": np.ascontiguousarray(L0_gnn_rel_pair_index),
        "wq_t": np.ascontiguousarray(np.asarray(L0_gnn_Wq).T),
        "bq": np.ascontiguousarray(L0_gnn_bq),
        "wk_t": np.ascontiguousarray(np.asarray(L0_gnn_Wk).T),
        "bk": np.ascontiguousarray(L0_gnn_bk),
    }
    nc = bacc.Bacc("TRN2", target_bir_lowering=False, num_devices=1)
    args = [nc.dram_tensor(f"in_{k}", a.shape, mybir.dt.from_np(a.dtype), kind="ExternalInput").ap() for k, a in laid_out.items()]
    out = nc.dram_tensor("out", (N, H), f32, kind="ExternalOutput").ap()
    build(nc, *args, out)
    r = run_bass_kernel_spmd(nc, [{f"in_{k}": a for k, a in laid_out.items()}], core_ids=[0])
    return r.results[0]["out"]
```

```python
import concourse.bass as bass
from concourse import mybir
from concourse.alu_op_type import AluOpType as ALU
from contextlib import ExitStack
import numpy as np

ACT = mybir.ActivationFunctionType
AX = mybir.AxisListType
f32, f16, i32 = mybir.dt.float32, mybir.dt.float16, mybir.dt.int32

P = 128
N, H = 1354, 512
HEADS = 8
DK = H // HEADS
E = 10000
C = -(-N // P)
NP = C * P
TAIL = N - (C - 1) * P
EC = -(-E // P)
EFULL = E // EC
EREST = E - EFULL * EC
HC = H // P
STAGES = 3
DIAG = 1e-7
EPS = 1e-5
E_ZERO = float(np.exp(-DIAG))
FAR = 1e30
XS, ZS = 2048.0, 64.0
EXPONENT = 0x7F800000
TOP = 127 + 14 + 127
GROUP_A = list(range(0, 6))
X_LOADS = [(0, 3), (3, 7), (7, C)]
BLOCK = 16
ECP = -(-EC // BLOCK) * BLOCK
HU = H + 3
PARTS = [(0, 6), (6, 9), (9, C)]
AHEAD = list(range(0, 5))
BESIDE = list(range(5, C))
STEPS_TO_RANKS, STEPS_TO_PACK = 6, 9
BEFORE_QK, AFTER_QK, IN_LOOP2, IN_LOOP3, IN_LOOP4 = 1, 1, 1, 1, 1
ROWS_V = (1, 3, 5)
ROWS_S = tuple(r for r in range(C) if r not in ROWS_V)
SUB, OBJ, USED, SUB1, KEY = range(5)
EX_S, EX_0, EX_D, EX_ONE, EX_FIRST, EX_N = 0, HEADS, 2 * HEADS, 3 * HEADS, 3 * HEADS + 1, 3 * HEADS + 2


class Steps:

    def __init__(self, eng, sem, base=0, by=1):
        self.eng, self.sem, self.base, self.by, self.n = eng, sem, base, by, 0

    def __call__(self, instruction):
        instruction.then_inc(self.sem, self.by)
        self.n += self.by
        self.eng.wait_ge(self.sem, self.base + self.n)


PACK_STEPS, SCORE_STEPS, LOOP2_STEPS, ROW_STEPS, LOOP3_STEPS, SUM_STEPS = 5, 3, 12, 12, 17, 3
LOOP4_STEPS, TOTAL_STEPS = 18, 2


def build(nc, x, adj, adj_t, pairs, wq_t, bq, wk_t, bk, out):
    ctx = ExitStack()
    with ctx:
        ctx.enter_context(nc.allow_non_contiguous_dma(reason="the adjacency's diagonal"))

        def sb(name, shape, dt):
            return ctx.enter_context(nc.sbuf_tensor(name, shape, dt))

        def sem(name):
            return ctx.enter_context(nc.semaphore(name))

        at = sb("at", [P, C, NP], f16)
        bm = sb("bm", [P, C, NP], f16)
        xs = sb("xs", [P, C, H], f32)
        u = sb("u", [P, C, HU], f32)
        terms = sb("terms", [P, 2, C, H], f16)
        work = sb("work", [P, ECP * P], f16)
        stage = sb("stage", [P, STAGES * NP], f32)
        gath = sb("gath", [P, 2, H], f32)
        gath_u = sb("gath_u", [P, HU], f32)
        gath_t = sb("gath_t", [P, 2, HC, P], f32)
        biases = sb("biases", [1, 2, H], f32)
        slot_cols = sb("slot_cols", [P, P, BLOCK], f16)
        rank16 = sb("rank16", [P, ECP], f16)
        dz = sb("dz", [P, 2, H], f16)

        onehot = work[:, :].rearrange("p (b s c) -> p b s c", s=P, c=BLOCK)
        words = work[:, :].bitcast(f32)
        diag = words[:, 0:10 * P].rearrange("p (h s) -> p h s", h=10)
        far = words[:, 10 * P:18 * P].rearrange("p (h s) -> p h s", h=HEADS)
        prod = words[:, 18 * P:18 * P + H]
        k_sb = words[:, 18 * P + H:18 * P + 2 * H]
        v_other = words[:, 18 * P + 2 * H:18 * P + 3 * H]
        row_x = words[:, 18 * P + 3 * H:18 * P + 4 * H]
        row_x0 = words[:, 18 * P + 4 * H:18 * P + 5 * H]
        stg = stage[:, :].rearrange("p (s n) -> p s n", s=STAGES)
        w_sb = stage[:, 0:2 * HC * H].rearrange("p (w c n) -> p w c n", w=2, c=HC)

        pair_rows = stage[:, 0:2 * N].rearrange("p (w n) -> p w n", w=2)
        bm_e = stage[:, 2 * N:2 * N + NP // 2].bitcast(f16)
        node_row = stage[:, 2 * N + NP // 2:2 * N + NP].bitcast(f16)

        ident = sb("ident", [P, P], f32)
        ident16 = sb("ident16", [P, P], f16)
        ones = sb("ones", [P, P], f32)
        ones16 = sb("ones16", [P, P], f16)
        above16 = sb("above16", [P, P], f16)
        slot_row = sb("slot_row", [P, P], f16)
        slot_id = sb("slot_id", [P, EC], f32)

        raw = sb("raw", [P, EC, 2], i32)
        pf = sb("pf", [P, EC, 2], f32)
        pg = sb("pg", [P, EC, 2], f32)
        ok = sb("ok", [P, EC], f32)
        ok2 = sb("ok2", [P, EC], f32)
        at_idx = sb("at_idx", [P, EC], i32)
        kept = sb("kept", [P, EC], f32)
        code = sb("code", [P, EC, 3], f16)
        rank = sb("rank", [P, EC], f32)
        onecol = sb("onecol", [P, EC], f32)
        total16 = sb("total16", [P, 1], f16)
        base = sb("base", [P, 2], f32)
        count_i = sb("count_i", [P, 2], i32)
        tiles_i = sb("tiles_i", [P, 1], i32)

        slots = sb("slots", [P, EC, 5], f32)
        scores = sb("scores", [P, EC, HEADS], f32)
        exps = sb("exps", [P, EC, EX_N], f32)
        so = sb("so", [P, 5], f32)
        so_i = sb("so_i", [P, 2], i32)
        row_i = sb("row_i", [P, 2], i32)
        other = sb("other", [P, 2], f32)
        ahead = sb("ahead", [P, 1], f32)
        earlier = sb("earlier", [P, 4], f32)
        slot_col = sb("slot_col", [P, P], f32)
        same = sb("same", [P, P], f32)
        same_row = sb("same_row", [P, P], f32)
        same_key = sb("same_key", [P, P], f32)
        s8 = sb("s8", [P, HEADS], f32)
        s_other = sb("s_other", [P, HEADS], f32)
        m8 = sb("m8", [P, HEADS], f32)
        m_new = sb("m_new", [P, HEADS], f32)
        ex = sb("ex", [P, EX_N], f32)
        ex_other = sb("ex_other", [P, EX_N], f32)
        z_sum = sb("z_sum", [P, EX_N], f32)
        zz = sb("zz", [P, HEADS], f32)
        shares = sb("shares", [P, 3, HEADS], f32)
        wcd = sb("wcd", [P, 3], f32)
        coef = sb("coef", [P, 5], f32)
        change = sb("change", [P, EC, 1], f32)
        spot = sb("spot", [P, 3], f32)
        spot_i = sb("spot_i", [P, 1], i32)
        one_z = sb("one_z", [P, C], f32)
        ratio = sb("ratio", [P, C], f32)
        a_ii = sb("a_ii", [P, C], f32)
        row_a = sb("row_a", [P, C], f32)
        col_a = sb("col_a", [P, C], f32)
        squares = sb("squares", [P, 2, C], f32)
        roots = sb("roots", [P, 2, C], f32)
        inverse = sb("inverse", [P, 2, C], f32)
        dinv_x = sb("dinv_x", [P, C], f32)
        dinv_z = sb("dinv_z", [P, C], f32)
        peak = sb("peak", [P, 5], f32)
        peak_i = sb("peak_i", [1, 4], i32)
        scale = sb("scale", [P, 2], f32)
        stats = sb("stats", [P, C, 6], f32)
        mv = sb("mv", [P, C, 2], f32)
        std = sb("std", [P, C], f32)
        rstd = sb("rstd", [P, C], f32)
        nmr = sb("nmr", [P, C], f32)
        warm = sb("warm", [P, 1], f32)
        eps_c = sb("eps_c", [P, 1], f32)

        ps = ctx.enter_context(nc.psum_tensor("ps", [P, 8, 512], f32))

        u_rows = nc.dram_tensor("u_rows", [N, HU], f32).ap()
        x1_rows = nc.dram_tensor("x1_rows", [N + P, H], f32).ap()
        v_rows = nc.dram_tensor("v_rows", [EC * P, H], f32).ap()

        pads = sem("pads")
        pairs_in = sem("pairs_in")
        x_in = [sem("x_in0"), sem("x_in1"), sem("x_in2")]
        aii_in = sem("aii_in")
        bias_in = sem("bias_in")
        w_in = sem("w_in")
        stage_in = [sem(f"stage_in{i}") for i in range(STAGES)]
        at_even = sem("at_even")
        at_odd = sem("at_odd")
        consts = sem("consts")
        pool_step = sem("pool_step")
        pool_passed = sem("pool_passed")
        idx_ready = sem("idx_ready")
        kept_in = sem("kept_in")
        peak_found = sem("peak_found")
        peak_row = sem("peak_row")
        scale_found = sem("scale_found")
        scale_row = sem("scale_row")
        scale_ready = sem("scale_ready")
        x_hi = sem("x_hi")
        x_lo = sem("x_lo")
        ax_done = sem("ax_done")
        ax_out = sem("ax_out")
        rows_s = sem("rows_s")
        rows_v = sem("rows_v")
        bm_ready = sem("bm_ready")
        v_step = sem("v_step")
        v_passed = sem("v_passed")
        base_in = sem("base_in")
        base_done = sem("base_done")
        tiles_ready = sem("tiles_ready")
        counts_ready = sem("counts_ready")
        u_stored = sem("u_stored")
        nodes_ready = sem("nodes_ready")
        x1_stored = sem("x1_stored")
        l1_step = sem("l1_step")
        score_step = sem("score_step")
        l1_onehot = sem("l1_onehot")
        l1_packed = sem("l1_packed")
        l1_slots = sem("l1_slots")
        idx_taken = sem("idx_taken")
        l1_sub = sem("l1_sub")
        l1_obj = sem("l1_obj")
        l1_turned = sem("l1_turned")
        l1_turned_sb = sem("l1_turned_sb")
        l1_k = sem("l1_k")
        l1_q = sem("l1_q")
        l1_k_sb = sem("l1_k_sb")
        l1_tile = sem("l1_tile")
        l2_step = sem("l2_step")
        row_step = sem("row_step")
        id_diag = sem("id_diag")
        id_row = sem("id_row")
        s_diag = sem("s_diag")
        s_row = sem("s_row")
        l2_arg = sem("l2_arg")
        l2_exp = sem("l2_exp")
        l3_step = sem("l3_step")
        sum_step = sem("sum_step")
        l3_diag = sem("l3_diag")
        l3_row = sem("l3_row")
        l3_same = sem("l3_same")
        l3_sum = sem("l3_sum")
        l3_sub = sem("l3_sub")
        l3_obj = sem("l3_obj")
        l3_u = sem("l3_u")
        l3_tile = sem("l3_tile")
        v_stored = sem("v_stored")
        prod_free = sem("prod_free")
        l4_step = sem("l4_step")
        total_step = sem("total_step")
        l4_diag = sem("l4_diag")
        l4_row = sem("l4_row")
        l4_same = sem("l4_same")
        l4_v = sem("l4_v")
        l4_sum = sem("l4_sum")
        l4_var = sem("l4_var")
        l4_root = sem("l4_root")
        l4_x1 = sem("l4_x1")
        l4_x0 = sem("l4_x0")
        l4_bm = sem("l4_bm")
        l4_dz = sem("l4_dz")
        l4_done = sem("l4_done")
        l4_added = sem("l4_added")
        l4_tile = sem("l4_tile")
        last_done = sem("last_done")
        last_added = sem("last_added")
        x1_fixed = sem("x1_fixed")
        row_free = sem("row_free")
        var0 = sem("var0")
        std0 = sem("std0")
        nmr_ready = sem("nmr_ready")
        bx_out = sem("bx_out")
        x1_in = sem("x1_in")
        s_passed = sem("s_passed")
        x1_ready = sem("x1_ready")
        xt_hi = sem("xt_hi")
        xt_lo = sem("xt_lo")
        bx_done = sem("bx_done")
        zt_hi = sem("zt_hi")
        zt_lo = sem("zt_lo")
        y_done = sem("y_done")
        warmed = sem("warmed")
        y_added = sem("y_added")
        var1 = sem("var1")
        std1 = sem("std1")
        scaled = sem("scaled")
        out_done = sem("out_done")

        x_rows = x[0:(C - 1) * P, :].rearrange("(c p) d -> p c d", p=P)
        adj_flat = adj_t.rearrange("a b -> (a b)").rearrange("(n o) -> n o", o=1)

        def ax_bank(i):
            return i if i < 8 else i - 3

        def rows_cast(eng, r):
            if r in ROWS_V:
                eng.wait_ge(rows_v, ROWS_V.index(r) + 1)
            else:
                eng.wait_ge(rows_s, ROWS_S.index(r) + 1)

        def loop_tiles(eng):
            eng.wait_ge(tiles_ready, 1)
            return eng.value_load(tiles_i[0:1, 0:1], min_val=1, max_val=EC)

        block = ctx.enter_context(nc.Block())

        @block.sync
        def _(sp):
            sp.wait_ge(pads, 1)
            sp.dma_start(raw[0:EFULL, :, :], pairs[0:EFULL * EC, :].rearrange("(p c) two -> p c two", c=EC)).then_inc(pairs_in, 16)
            sp.dma_start(raw[EFULL:EFULL + 1, 0:EREST, :],
                         pairs[EFULL * EC:E, :].rearrange("(p c) two -> p c two", p=1)).then_inc(pairs_in, 16)
            sp.wait_ge(pads, 6)
            for (lo, hi), arrived in zip(X_LOADS, x_in):
                full = min(hi, C - 1)
                sp.dma_start(xs[:, lo:full, :], x_rows[:, lo:full, :]).then_inc(arrived, 16)
            sp.dma_start(xs[0:TAIL, C - 1, :], x[(C - 1) * P:N, :]).then_inc(x_in[-1], 16)
            for k in range(C):
                if k >= STAGES:
                    j = k - STAGES
                    sp.wait_ge(at_odd if j % 2 else at_even, j // 2 + 1)
                rows = P if k < C - 1 else TAIL
                sp.dma_start(stg[0:rows, k % STAGES, 0:N], adj_t[k * P:k * P + rows, :]).then_inc(stage_in[k % STAGES], 16)
            sp.dma_start(a_ii[:, 0:C - 1].rearrange("p (c o) -> p c o", o=1), bass.AP(tensor=adj_t.tensor, offset=0, ap=[[N + 1, P], [P * (N + 1), C - 1], [1, 1]])).then_inc(aii_in, 16)
            sp.dma_start(a_ii[0:TAIL, C - 1:C],
                         bass.AP(tensor=adj_t.tensor, offset=(C - 1) * P * (N + 1), ap=[[N + 1, TAIL], [1, 1]])).then_inc(aii_in, 16)
            sp.dma_start(biases[0:1, 0, :], bq.rearrange("(o n) -> o n", o=1)).then_inc(bias_in, 16)
            sp.dma_start(biases[0:1, 1, :], bk.rearrange("(o n) -> o n", o=1)).then_inc(bias_in, 16)
            for r in range(C):
                n = C + r
                j = n - STAGES
                if j < C:
                    sp.wait_ge(at_odd if j % 2 else at_even, j // 2 + 1)
                else:
                    rows_cast(sp, j - C)
                rows = P if r < C - 1 else TAIL
                sp.dma_start(stg[0:rows, n % STAGES, 0:N], adj[r * P:r * P + rows, :]).then_inc(stage_in[n % STAGES], 16)
            sp.wait_ge(rows_s, len(ROWS_S))
            sp.wait_ge(rows_v, len(ROWS_V))
            sp.dma_start(w_sb[:, 0, :, :], wq_t.rearrange("(c p) n -> p c n", p=P)).then_inc(w_in, 16)
            sp.dma_start(w_sb[:, 1, :, :], wk_t.rearrange("(c p) n -> p c n", p=P)).then_inc(w_in, 16)
            for m, (lo, hi) in enumerate(PARTS):
                sp.wait_ge(counts_ready, m + 1)
                for i in range(lo, hi):
                    rows = P if i < C - 1 else TAIL
                    sp.dma_start(u_rows[i * P:i * P + rows, :], u[0:rows, i, :]).then_inc(u_stored, 16)
                for i in range(lo, hi):
                    rows = P if i < C - 1 else TAIL
                    sp.wait_ge(x1_ready, i + 1)
                    sp.dma_start(x1_rows[i * P:i * P + rows, :], xs[0:rows, i, :]).then_inc(x1_stored, 16)
            tiles = loop_tiles(sp)
            sp.wait_ge(x1_fixed, tiles * 16)
            sp.sem_inc(s_passed, 1)
            sp.wait_ge(xt_lo, C)
            for i in range(C):
                rows = P if i < C - 1 else TAIL
                sp.dma_start(xs[0:rows, i, :], x1_rows[i * P:i * P + rows, :]).then_inc(x1_in, 16)
            for i in range(C):
                rows = P if i < C - 1 else TAIL
                sp.wait_ge(scaled, i + 1)
                sp.dma_start(out[i * P:i * P + rows, :], xs[0:rows, i, :]).then_inc(out_done, 16)
            sp.wait_ge(out_done, 16 * C)

        @block.gpsimd
        def _(pool):
            step = Steps(pool, pool_step)
            for t in (ident, ident16, above16):
                v = 1.0 if t is above16 else 0.0
                pool.memset(t[:, :], v).then_inc(pool_step, 1)
                step.n += 1
            pool.wait_ge(pool_step, step.n)
            for t in (ident, ident16):
                pool.affine_select(out=t[:, :], in_=t[:, :], compare_op=ALU.not_equal, fill=1.0, base=0,
                                   pattern=[[-1, P]], channel_multiplier=1).then_inc(consts, 1)
            pool.affine_select(out=above16[:, :], in_=above16[:, :], compare_op=ALU.is_gt, fill=0.0, base=0,
                               pattern=[[1, P]], channel_multiplier=-1).then_inc(consts, 1)
            imp = dict(allow_small_or_imprecise_dtypes=True)
            pool.iota(slot_row[:, :], pattern=[[1, P]], base=1, channel_multiplier=0, **imp).then_inc(consts, 1)
            pool.iota(slot_id[:, :], pattern=[[P, EC]], base=0, channel_multiplier=1, **imp).then_inc(consts, 1)
            pool.iota(slot_col[:, :], pattern=[[1, P]], base=0, channel_multiplier=0, **imp).then_inc(consts, 1)
            pool.wait_ge(idx_ready, 1)
            for c in range(EC):
                pool.indirect_dma_start(out=kept[:, c:c + 1], out_offset=None, in_=adj_flat,
                                        in_offset=bass.IndirectOffsetOnAxis(ap=at_idx[:, c:c + 1], axis=0)).then_inc(kept_in, 16)
            def pool_wait(signal, value):
                pool.wait_ge(signal, value)
                pool.sem_inc(pool_passed, 1)

            tiles = loop_tiles(pool)

            def take_indices(t, n, into=so_i):
                pool.tensor_copy(into[:, :], slots[:, bass.ds(t, 1), 0:2].rearrange("p o f -> p (o f)")).then_inc(idx_taken, 1)
                pool_wait(idx_taken, n)

            def gather_x(w, done):
                pool.indirect_dma_start(out=gath[:, w, :], out_offset=None, in_=x,
                                        in_offset=bass.IndirectOffsetOnAxis(ap=so_i[:, w:w + 1], axis=0)).then_inc(done, 16)

            with pool.Fori(0, tiles) as t:
                pool_wait(l1_slots, t + 1)
                take_indices(t, t + 1)
                gather_x(1, l1_obj)
                gather_x(0, l1_sub)
                pool_wait(l1_tile, t + 2)

            def gather_rows():
                for dst, matrix, done in ((row_x0, x1_rows[0:N, :], l4_x0), (pair_rows[:, 0, :], adj, l4_bm), (pair_rows[:, 1, :], adj_t, l4_bm)):
                    pool.indirect_dma_start(out=dst, out_offset=None, in_=matrix,
                                            in_offset=bass.IndirectOffsetOnAxis(ap=row_i[:, 0:1], axis=0)).then_inc(done, 16)

            pool.iota(node_row, pattern=[[1, NP]], base=0, channel_multiplier=0, **imp).then_inc(nodes_ready, 1)
            pool.wait_ge(x1_stored, 16 * C)
            pool.wait_ge(u_stored, 16 * C)
            take_indices(0, tiles + 1, row_i)
            gather_rows()
            with pool.Fori(0, tiles) as t:
                take_indices(t, tiles + t + 2)
                pool.indirect_dma_start(out=gath_u[:, :], out_offset=None, in_=u_rows,
                                        in_offset=bass.IndirectOffsetOnAxis(ap=so_i[:, 0:1], axis=0)).then_inc(l3_u, 16)
                gather_x(1, l3_obj)
                gather_x(0, l3_sub)
                pool_wait(l3_tile, t + 1)
                pool.dma_start(v_rows[bass.ts(t, P), :], prod).then_inc(v_stored, 16)
                pool_wait(v_stored, t * 16 + 16)
                pool.sem_inc(prod_free, 1)
            with pool.Fori(0, tiles) as t:
                pool_wait(l4_tile, t + 1)
                with pool.If(t > 0):
                    take_indices(t, tiles * 2 + t + 1, row_i)
                    gather_rows()
                with pool.Fori(0, tiles) as o:
                    pool.dma_start(v_other, v_rows[bass.ts(o, P), :]).then_inc(l4_v, 16)
                    pool_wait(l4_sum, t * tiles + o + 1)
                pool_wait(l4_x0, t * 16 + 16)
                pool_wait(l4_x1, t + 1)
                pool.indirect_dma_start(out=x1_rows, out_offset=bass.IndirectOffsetOnAxis(ap=spot_i[:, 0:1], axis=0),
                                        in_=row_x, in_offset=None).then_inc(x1_fixed, 16)
                pool_wait(x1_fixed, t * 16 + 16)
                pool.sem_inc(row_free, 1)

        @block.scalar
        def _(act):
            act.wait_ge(scale_ready, 1)
            for k in range(C):
                act.activation(terms[:, 0, k, :], xs[:, k, :], ACT.Copy, scale=scale[:, 0:1]).then_inc(x_hi, 1)
                if k % 2 == 0:
                    act.wait_ge(stage_in[k % STAGES], 16 * (k // STAGES + 1))
                    rows = P if k < C - 1 else TAIL
                    if k == C - 1:
                        act.wait_ge(pads, 11)
                    act.activation(at[0:rows, k, 0:N], stg[0:rows, k % STAGES, 0:N], ACT.Copy,
                                   accum_out=col_a[0:rows, k:k + 1]).then_inc(at_even, 1)

            def ax_evacuate(i, bank):
                act.wait_ge(ax_done, i + 1)
                act.activation(u[:, i, 0:H], ps[:, bank, :], ACT.Copy, scale=scale[:, 1:2]).then_inc(ax_out, 1)

            def adj_rows(r):
                n = C + r
                rows = P if r < C - 1 else TAIL
                act.wait_ge(stage_in[n % STAGES], 16 * (n // STAGES + 1))
                act.activation(bm[0:rows, r, 0:N], stg[0:rows, n % STAGES, 0:N], ACT.Copy,
                               accum_out=row_a[0:rows, r:r + 1]).then_inc(rows_s, 1)

            for r in (0, 2, 4):
                adj_rows(r)
            for i in GROUP_A:
                ax_evacuate(i, i)
            def roots_of(m):
                lo, hi = PARTS[m]
                act.wait_ge(var0, m + 1)
                act.activation(roots[:, :, lo:hi], squares[:, :, lo:hi], ACT.Sqrt).then_inc(std0, 1)

            def dense_norm(m):
                act.wait_ge(nmr_ready, m + 1)
                for i in range(*PARTS[m]):
                    act.activation(xs[:, i, :], xs[:, i, :], ACT.Identity, scale=inverse[:, 0, i:i + 1],
                                   bias=nmr[:, i:i + 1]).then_inc(x1_ready, 1)

            def high_terms(m):
                act.wait_ge(x1_ready, PARTS[m][1])
                for i in range(*PARTS[m]):
                    act.activation(terms[:, 0, i, :], xs[:, i, :], ACT.Copy, scale=dinv_x[:, i:i + 1]).then_inc(xt_hi, 1)

            adj_rows(6)
            adj_rows(7)
            adj_rows(8)
            ax_evacuate(6, ax_bank(6))
            adj_rows(9)
            adj_rows(10)
            ax_evacuate(7, ax_bank(7))
            roots_of(0)
            dense_norm(0)
            ax_evacuate(8, ax_bank(8))
            ax_evacuate(9, ax_bank(9))
            ax_evacuate(10, ax_bank(10))
            high_terms(0)
            roots_of(1)
            dense_norm(1)
            high_terms(1)
            roots_of(2)
            dense_norm(2)
            high_terms(2)
            def bx_evacuate(i):
                act.wait_ge(bx_done, i + 1)
                act.activation(u[:, i, 0:H], ps[:, i % 5, :], ACT.Copy).then_inc(bx_out, 1)

            act.wait_ge(u_stored, 16 * C)
            bx_evacuate(0)
            act.activation(warm[:, :], eps_c[:, :], ACT.Exp).then_inc(warmed, 1)
            tiles = loop_tiles(act)
            with act.Fori(0, tiles) as t:
                for w in range(2):
                    act.wait_ge(l1_turned, 2 * t + w + 1)
                    act.activation(gath_t[:, 1 - w, :, :], ps[:, 7 if w else 5, :].rearrange("p (c s) -> p c s", c=HC),
                                   ACT.Copy).then_inc(l1_turned_sb, 1)
                act.wait_ge(l1_k, t + 1)
                act.activation(k_sb, ps[:, 6, :], ACT.Copy).then_inc(l1_k_sb, 1)
            for i in AHEAD[1:]:
                bx_evacuate(i)
            with act.Fori(0, tiles) as t:
                act.wait_ge(l2_arg, t + 1)
                act.activation(ex[:, 0:3 * HEADS], ex[:, 0:3 * HEADS], ACT.Exp).then_inc(l2_exp, 1)
            act.activation(warm[:, :], warm[:, :], ACT.Sqrt).then_inc(warmed, 1)
            for i in BESIDE[:-IN_LOOP4]:
                bx_evacuate(i)
            with act.Fori(0, tiles) as t:
                act.wait_ge(l4_var, t + 1)
                act.activation(coef[:, 4:5], coef[:, 3:4], ACT.Sqrt, bias=eps_c[:, 0:1]).then_inc(l4_root, 1)
                with act.If(t < 1):
                    for i in BESIDE[-IN_LOOP4:]:
                        bx_evacuate(i)
            for i in range(C):
                act.wait_ge(last_added, i + 1)
                act.activation(terms[:, 0, i, :], u[:, i, 0:H], ACT.Copy, scale=dinv_z[:, i:i + 1]).then_inc(zt_hi, 1)
            for i in range(C):
                act.wait_ge(var1, i + 1)
                act.activation(std[:, i:i + 1], mv[:, i, 1:2], ACT.Sqrt, bias=eps_c[:, 0:1]).then_inc(std1, 1)

        @block.tensor
        def _(pe):
            def together_step(k, first, last, bank_free, ready, matrix, done, chunks=GROUP_A):
                ready(k)
                for i in chunks:
                    if first:
                        bank_free(i)
                    for s in range(2):
                        m = pe.matmul(ps[:, i, :], matrix[:, k, i * P:(i + 1) * P], terms[:, s, k, :],
                                      start=first and s == 0, stop=last and s == 1)
                    if last:
                        m.then_inc(done, 1)

            def in_turn(first, last, bank_free, bank_of, matrix, done):
                def one_chunk(i):
                    bank_free(i)
                    for k in range(C):
                        for s in range(2):
                            m = pe.matmul(ps[:, bass.ds(bank_of(i), 1), :].rearrange("p o d -> p (o d)"),
                                          matrix[:, k, bass.ts(i, P)], terms[:, s, k, :],
                                          start=(k == 0 and s == 0), stop=(k == C - 1 and s == 1))
                    m.then_inc(done, 1)

                if last - first == 1:
                    one_chunk(first)
                else:
                    with pe.Fori(first, last) as i:
                        one_chunk(i)

            pe.wait_ge(consts, 6)
            pe.wait_ge(peak_found, 1)
            pe.transpose(ps[0:1, 7, 0:P], peak[:, 0:1], ident[:, :]).then_inc(peak_row, 1)
            pe.wait_ge(pads, 11)
            pe.wait_ge(scale_found, 1)
            pe.matmul(ps[:, 7, P:P + 2], ones[0:1, :], peak_i[0:1, 2:4].bitcast(f32), start=True, stop=True).then_inc(scale_row, 1)

            for k in range(C):
                pe.wait_ge(at_odd if k % 2 else at_even, k // 2 + 1)
                together_step(k, k == 0, k == C - 1, lambda i: None, lambda k: pe.wait_ge(x_lo, k + 1), at, ax_done)

            in_turn(6, 8, lambda i: None, lambda i: i, at, ax_done)
            in_turn(8, C, lambda i: pe.wait_ge(ax_out, i - 2), lambda i: i - 3, at, ax_done)
            pe.wait_ge(ax_out, 5)

            def bx_step(k):
                together_step(k, k == 0, k == C - 1, lambda i: None, lambda k: pe.wait_ge(xt_lo, k + 1), bm, bx_done, AHEAD)

            def bx_chunks(first, n):
                for i in BESIDE[first:first + n]:
                    in_turn(i, i + 1, lambda i: pe.wait_ge(bx_out, i - 4), lambda i: i % 5, bm, bx_done)

            for k in range(0, STEPS_TO_RANKS):
                pe.wait_ge(bm_ready, k + 1)
                bx_step(k)
            pe.wait_ge(base_in, 1)
            pe.wait_ge(ax_out, C)
            pe.matmul(ps[:, 5, 0:1], above16[:, :], total16[:, :], start=True, stop=True)
            pe.matmul(ps[:, 5, 1:2], ones16[:, :], total16[:, :], start=True, stop=True).then_inc(base_done, 1)

            pe.wait_ge(bm_ready, C)
            for k in range(STEPS_TO_RANKS, STEPS_TO_PACK):
                bx_step(k)
            tiles = loop_tiles(pe)
            with pe.Fori(0, tiles) as t:
                for c in range(EC):
                    if c % BLOCK == 0:
                        pe.wait_ge(l1_onehot, t * (ECP // BLOCK) + c // BLOCK + 1)
                    m = pe.matmul(ps[:, 7, 0:3], onehot[:, c // BLOCK, :, c % BLOCK], code[:, c, :], start=(c == 0), stop=(c == EC - 1))
                m.then_inc(l1_packed, 1)
            pe.wait_ge(w_in, 32)
            pe.wait_ge(bias_in, 32)
            for k in range(STEPS_TO_PACK, C):
                bx_step(k)
            pe.wait_ge(l1_slots, tiles)
            bx_chunks(0, BEFORE_QK)
            with pe.Fori(0, tiles) as t:
                pe.wait_ge(l1_tile, t + 1)
                for w, got in ((1, l1_obj), (0, l1_sub)):
                    pe.wait_ge(got, 16 * t + 16)
                    for c in range(HC):
                        m = pe.transpose(ps[:, 5 if w else 7, c * P:(c + 1) * P], gath[:, w, c * P:(c + 1) * P], ident[:, :])
                    m.then_inc(l1_turned, 1)
                for n, (w, done) in enumerate(((1, l1_k), (0, l1_q))):
                    pe.matmul(ps[:, 5 + w, :], ones[0:1, :], biases[0:1, w, :], start=True, stop=False)
                    pe.wait_ge(l1_turned_sb, 2 * t + 1 + n)
                    for c in range(HC):
                        m = pe.matmul(ps[:, 5 + w, :], gath_t[:, w, c, :], w_sb[:, w, c, :], start=False, stop=(c == HC - 1))
                    m.then_inc(done, 1)
            bx_chunks(BEFORE_QK, AFTER_QK)
            with pe.Fori(0, tiles) as t:
                with pe.Fori(0, tiles) as o:
                    pe.wait_ge(id_diag, t * tiles + o + 1)
                    pe.matmul(ps[:, 7, 0:2 * P], ones[:, :], words[:, 8 * P:10 * P], start=True, stop=True).then_inc(id_row, 1)
                    pe.wait_ge(s_diag, t * tiles + o + 1)
                    for g in range(2):
                        m = pe.matmul(ps[:, 5 + g, :], ones[:, :], words[:, g * 512:(g + 1) * 512], start=True, stop=True)
                    m.then_inc(s_row, 1)

                with pe.If(t < 1):
                    bx_chunks(BEFORE_QK + AFTER_QK, IN_LOOP2)

            with pe.Fori(0, tiles) as t:
                pe.wait_ge(l3_diag, t + 1)
                pe.matmul(ps[:, 7, 0:P], ones[:, :], diag[:, 8, :], start=True, stop=True).then_inc(l3_row, 1)
                with pe.Fori(0, tiles) as o:
                    pe.wait_ge(l3_same, t * tiles + o + 1)
                    pe.matmul(ps[:, 6, 0:EX_N], same[:, :], ex_other[:, :], start=True, stop=True).then_inc(l3_sum, 1)
                with pe.If(t < 1):
                    bx_chunks(BEFORE_QK + AFTER_QK + IN_LOOP2, IN_LOOP3)
            placed = BEFORE_QK + AFTER_QK + IN_LOOP2 + IN_LOOP3
            bx_chunks(placed, len(BESIDE) - placed - IN_LOOP4)

            def change_product(c, done, added, before):
                if c >= 2:
                    pe.wait_ge(added, before + c - 1)
                for s in range(2):
                    m = pe.matmul(ps[:, 6 + c % 2, :], bm_e[:, c * P:(c + 1) * P], dz[:, s, :], start=(s == 0), stop=(s == 1))
                m.then_inc(done, 1)

            with pe.Fori(0, tiles) as t:
                with pe.If(t > 0):
                    pe.wait_ge(l4_dz, t + 1)
                    for c in range(C):
                        change_product(c, l4_done, l4_added, t * C)
                pe.wait_ge(l4_diag, t + 1)
                pe.matmul(ps[:, 7, 0:P], ones[:, :], diag[:, 8, :], start=True, stop=True).then_inc(l4_row, 1)
                with pe.Fori(0, tiles) as o:
                    pe.wait_ge(l4_v, (t * tiles + o) * 16 + 16)
                    pe.wait_ge(l4_same, t * tiles + o + 1)
                    pe.matmul(ps[:, 6, :], same[:, :], v_other, start=True, stop=True).then_inc(l4_sum, 1)
                with pe.If(t < 1):
                    bx_chunks(len(BESIDE) - IN_LOOP4, IN_LOOP4)
            pe.wait_ge(l4_dz, tiles + 1)
            change_product(0, last_done, last_added, 0)
            change_product(1, last_done, last_added, 0)
            pe.wait_ge(bx_out, C)
            for k in range(C):
                if k + 2 < C:
                    change_product(k + 2, last_done, last_added, 0)
                together_step(k, k == 0, k == C - 1, lambda i: None, lambda k: pe.wait_ge(zt_lo, k + 1), at, y_done)
            pe.wait_ge(last_added, C)
            in_turn(6, 8, lambda i: None, lambda i: i, at, y_done)
            in_turn(8, C, lambda i: pe.wait_ge(y_added, i - 7), lambda i: i - 8, at, y_done)

        @block.vector
        def _(dve):
            main = Steps(dve, v_step)
            dve.memset(raw[:, :, :], N).then_inc(pads, 1)
            dve.memset(xs[:, C - 1, :], 0.0).then_inc(pads, 1)
            dve.memset(a_ii[:, :], 0.0).then_inc(pads, 1)
            dve.memset(col_a[:, C - 1:C], 0.0).then_inc(pads, 1)
            dve.memset(row_a[:, C - 1:C], 0.0).then_inc(pads, 1)
            dve.memset(eps_c[:, :], EPS).then_inc(pads, 1)
            dve.memset(at[:, C - 1, :], 0.0).then_inc(pads, 1)
            dve.memset(at[:, 0:C - 1, N:NP], 0.0).then_inc(pads, 1)
            dve.memset(bm[:, C - 1, :], 0.0).then_inc(pads, 1)
            dve.memset(bm[:, 0:C - 1, N:NP], 0.0).then_inc(pads, 1)
            dve.memset(ones[:, :], 1.0).then_inc(pads, 1)
            dve.sem_inc(prod_free, 1)
            dve.sem_inc(row_free, 1)
            dve.sem_inc(l1_tile, 1)
            dve.sem_inc(l4_dz, 1)
            dve.sem_inc(l4_done, C)
            dve.sem_inc(l4_added, C)
            main(dve.memset(ones16[:, :], 1.0))
            main(dve.memset(onecol[:, :], 1.0))
            main(dve.memset(rank16[:, :], 0.0))
            dve.wait_ge(pairs_in, 32)
            main(dve.tensor_copy(pf[:, :, :], raw[:, :, :]))
            main(dve.tensor_scalar(pg[:, :, :], pf[:, :, :], 0.0, float(N), ALU.is_lt, ALU.mult))
            main(dve.tensor_tensor(pf[:, :, :], pf[:, :, :], pg[:, :, :], ALU.add))
            main(dve.tensor_scalar(pg[:, :, :], pf[:, :, :], 0.0, None, ALU.is_ge))
            main(dve.scalar_tensor_tensor(pg[:, :, :], pf[:, :, :], float(N), pg[:, :, :], ALU.is_lt, ALU.mult))
            main(dve.tensor_tensor(ok[:, :], pg[:, :, 0], pg[:, :, 1], ALU.mult))
            main(dve.tensor_tensor(ok2[:, :], pf[:, :, 0], pf[:, :, 1], ALU.not_equal))
            main(dve.tensor_tensor(ok[:, :], ok[:, :], ok2[:, :], ALU.mult))
            main(dve.scalar_tensor_tensor(ok2[:, :], pf[:, :, 1], float(N), pf[:, :, 0], ALU.mult, ALU.add))
            dve.tensor_tensor(at_idx[:, :], ok2[:, :], ok[:, :], ALU.mult).then_inc(idx_ready, 1)
            main(dve.tensor_tensor(code[:, :, 0], pf[:, :, 0], ok[:, :], ALU.mult))
            main(dve.tensor_tensor(code[:, :, 1], pf[:, :, 1], ok[:, :], ALU.mult))
            main(dve.tensor_copy(code[:, :, 2], ok[:, :]))
            for n, ((lo, hi), arrived) in enumerate(zip(X_LOADS, x_in)):
                dve.wait_ge(arrived, 32 if hi == C else 16)
                dve.tensor_reduce(peak[:, 1 + n:2 + n], xs[:, lo:hi, :].rearrange("p c d -> p (c d)"), AX.X, ALU.max,
                                  apply_absolute_value=True).then_inc(v_step, 1)
            main.n += len(X_LOADS)
            dve.wait_ge(v_step, main.n)
            dve.tensor_reduce(peak[:, 0:1], peak[:, 1:1 + len(X_LOADS)], AX.X, ALU.max).then_inc(peak_found, 1)
            dve.wait_ge(peak_row, 1)
            main(dve.tensor_reduce(peak[0:1, 4:5], ps[0:1, 7, 0:P], AX.X, ALU.max))
            main(dve.tensor_scalar(peak_i[:, 0:1], peak[0:1, 4:5].bitcast(i32), EXPONENT, None, ALU.bitwise_and))
            main(dve.tensor_scalar(peak_i[:, 1:2], peak_i[:, 0:1], float(32 << 23), None, ALU.max))
            main(dve.tensor_scalar(peak_i[:, 2:3], peak_i[:, 1:2], -1.0, float(TOP << 23), ALU.mult, ALU.add))
            dve.tensor_scalar(peak_i[:, 3:4], peak_i[:, 1:2], float((254 - TOP) * (1 << 23)), None, ALU.add).then_inc(scale_found, 1)
            dve.wait_ge(scale_row, 1)
            dve.tensor_copy(scale[:, :], ps[:, 7, P:P + 2]).then_inc(scale_ready, 1)
            dve.wait_ge(scale_ready, 1)
            for k in range(C):
                if k % 2:
                    dve.wait_ge(stage_in[k % STAGES], 16 * (k // STAGES + 1))
                    dve.tensor_scalar(at[:, k, 0:N], stg[:, k % STAGES, 0:N], 1.0, 0.0, ALU.mult, ALU.add,
                                      accum_out=col_a[:, k:k + 1]).then_inc(at_odd, 1)
                dve.wait_ge(x_hi, k + 1)
                dve.scalar_tensor_tensor(terms[:, 1, k, :], xs[:, k, :], scale[:, 0:1], terms[:, 0, k, :],
                                         ALU.mult, ALU.subtract).then_inc(x_lo, 1)
            dve.wait_ge(consts, 6)
            main(dve.tensor_copy(slot_cols[:, :, :], slot_row[:, :].rearrange("p (s o) -> p s o", o=1).to_broadcast([P, P, BLOCK])))
            dve.wait_ge(aii_in, 32)

            def dense_finish(m):
                lo, hi = PARTS[m]
                dve.wait_ge(std0, m + 1)
                main(dve.reciprocal(inverse[:, :, lo:hi], roots[:, :, lo:hi]))
                dve.tensor_scalar(dinv_x[:, lo:hi], inverse[:, 1, lo:hi], XS, None, ALU.mult).then_inc(v_step, 1)
                dve.tensor_scalar(dinv_z[:, lo:hi], inverse[:, 1, lo:hi], 0.5 * ZS / XS, None, ALU.mult).then_inc(v_step, 1)
                dve.scalar_tensor_tensor(nmr[:, lo:hi], mv[:, lo:hi, 0], -1.0, inverse[:, 0, lo:hi], ALU.mult, ALU.mult).then_inc(v_step, 1)
                dve.tensor_scalar(u[:, lo:hi, H + 2], inverse[:, 1, lo:hi], XS, None, ALU.mult).then_inc(v_step, 1)
                main.n += 4
                dve.wait_ge(v_step, main.n)
                dve.sem_inc(nmr_ready, 1)
                dve.sem_inc(counts_ready, 1)

            def low_term(i):
                dve.wait_ge(xt_hi, i + 1)
                dve.scalar_tensor_tensor(terms[:, 1, i, :], xs[:, i, :], dinv_x[:, i:i + 1], terms[:, 0, i, :],
                                         ALU.mult, ALU.subtract).then_inc(xt_lo, 1)

            def two_way(first, last):
                for r in range(first, last):
                    if r in ROWS_V:
                        n = C + r
                        dve.wait_ge(stage_in[n % STAGES], 16 * (n // STAGES + 1))
                        dve.tensor_scalar(bm[:, r, 0:N], stg[:, n % STAGES, 0:N], 1.0, 0.0, ALU.mult, ALU.add,
                                          accum_out=row_a[:, r:r + 1]).then_inc(rows_v, 1)
                    rows_cast(dve, r)
                    main(dve.tensor_tensor(bm[:, r, :], bm[:, r, :], at[:, r, :], ALU.add))
                    dve.scalar_tensor_tensor(bm[:, r, r * P:(r + 1) * P], ident16[:, :], 2.0, bm[:, r, r * P:(r + 1) * P],
                                             ALU.mult, ALU.add).then_inc(bm_ready, 1)

            def dense_rows(m):
                lo, hi = PARTS[m]
                dve.tensor_tensor(col_a[:, lo:hi], col_a[:, lo:hi], row_a[:, lo:hi], ALU.add).then_inc(v_step, 1)
                main.n += 1
                main(dve.tensor_tensor(row_a[:, lo:hi], row_a[:, lo:hi], a_ii[:, lo:hi], ALU.subtract))
                dve.tensor_copy(u[:, lo:hi, H], row_a[:, lo:hi]).then_inc(v_step, 1)
                dve.tensor_copy(u[:, lo:hi, H + 1], a_ii[:, lo:hi]).then_inc(v_step, 1)
                dve.tensor_scalar(squares[:, 1, lo:hi], col_a[:, lo:hi], 0.5, 1.0, ALU.mult, ALU.add).then_inc(v_step, 1)
                main.n += 3
                main(dve.tensor_scalar(one_z[:, lo:hi], row_a[:, lo:hi], E_ZERO, 1.0, ALU.mult, ALU.add))
                main(dve.tensor_scalar(ratio[:, lo:hi], one_z[:, lo:hi], 1.0, 1.0 / E_ZERO, ALU.add, ALU.mult))
                main(dve.tensor_tensor(ratio[:, lo:hi], ratio[:, lo:hi], a_ii[:, lo:hi], ALU.subtract))
                dve.wait_ge(x_lo, C)
                for i in range(lo, hi):
                    dve.wait_ge(ax_out, i + 1)
                    dve.scalar_tensor_tensor(xs[:, i, :], xs[:, i, :], ratio[:, i:i + 1], u[:, i, 0:H], ALU.mult, ALU.add).then_inc(v_step, 1)
                main.n += hi - lo
                for i in range(lo, hi):
                    dve.wait_ge(v_step, main.n)
                    dve.bn_stats(stats[:, i, :], xs[:, i, :]).then_inc(v_step, 1)
                main.n += hi - lo
                for i in range(lo, hi):
                    dve.wait_ge(v_step, main.n)
                    dve.bn_aggr(mv[:, i, :], stats[:, i, :]).then_inc(v_step, 1)
                main.n += hi - lo
                main(dve.tensor_scalar(one_z[:, lo:hi], one_z[:, lo:hi], EPS ** 0.5 / E_ZERO, None, ALU.mult))
                main(dve.tensor_tensor(one_z[:, lo:hi], one_z[:, lo:hi], one_z[:, lo:hi], ALU.mult))
                dve.tensor_tensor(squares[:, 0, lo:hi], mv[:, lo:hi, 1], one_z[:, lo:hi], ALU.add).then_inc(var0, 1)

            def low_terms(first, last):
                for i in range(first, last):
                    low_term(i)

            two_way(0, 6)
            dense_rows(0)
            two_way(6, C)
            dense_finish(0)
            dense_rows(1)
            low_terms(0, 2)
            dense_finish(1)
            low_terms(2, 4)
            dense_rows(2)
            low_terms(4, 7)
            dense_finish(2)
            low_terms(7, C)
            dve.wait_ge(kept_in, 16 * EC)
            main(dve.scalar_tensor_tensor(ok[:, :], kept[:, :], 1.0, ok[:, :], ALU.is_equal, ALU.mult))
            main(dve.tensor_tensor_scan(rank[:, :], onecol[:, :], ok[:, :], 0.0, ALU.mult, ALU.add))
            dve.tensor_copy(total16[:, :], rank[:, EC - 1:EC]).then_inc(base_in, 1)
            dve.wait_ge(base_done, 1)
            main(dve.tensor_copy(base[:, :], ps[:, 5, 0:2]))
            main(dve.scalar_tensor_tensor(rank[:, :], rank[:, :], base[:, 0:1], ok[:, :], ALU.add, ALU.mult))
            main(dve.tensor_scalar(count_i[:, 0:1], base[:, 1:2], 1.0, float(P - 1), ALU.max, ALU.add))
            dve.tensor_scalar(tiles_i[:, :], count_i[:, 0:1], 7, None, ALU.logical_shift_right).then_inc(tiles_ready, 1)
            tiles = loop_tiles(dve)

            def held(t, table):
                return table[:, bass.ds(t, 1), :].rearrange("p o f -> p (o f)")

            def spread(columns, n):
                return columns.rearrange("p (h o) -> p h o", o=1).to_broadcast([P, n, P])

            def eyes(n):
                return ident[:, :].rearrange("p (o s) -> p o s", o=1).to_broadcast([P, n, P])

            with dve.Fori(0, tiles) as t:
                step = Steps(dve, l1_step, t * PACK_STEPS)
                step(dve.tensor_copy(rank16[:, 0:EC], rank[:, :]))
                for b in range(ECP // BLOCK):
                    dve.tensor_tensor(onehot[:, b, :, :],
                                      rank16[:, b * BLOCK:(b + 1) * BLOCK].rearrange("p (o c) -> p o c", o=1).to_broadcast([P, P, BLOCK]),
                                      slot_cols[:, :, :], ALU.is_equal).then_inc(l1_onehot, 1)
                dve.wait_ge(l1_packed, t + 1)
                step(dve.tensor_copy(so[:, 0:3], ps[:, 7, 0:3]))
                dve.scalar_tensor_tensor(so[:, KEY:KEY + 1], so[:, SUB:SUB + 1], float(N), so[:, OBJ:OBJ + 1],
                                         ALU.mult, ALU.add).then_inc(l1_step, 1)
                step.n += 1
                step(dve.tensor_scalar(so[:, SUB1:SUB1 + 1], so[:, SUB:SUB + 1], so[:, USED:USED + 1], -1.0, ALU.add, ALU.add))
                dve.tensor_copy(held(t, slots), so[:, :]).then_inc(l1_slots, 1)
                step(dve.tensor_scalar(rank[:, :], rank[:, :], -float(P), None, ALU.add))
                assert step.n == PACK_STEPS, step.n
                dve.wait_ge(l1_slots, t + 1)

            with dve.Fori(0, tiles) as t:
                step = Steps(dve, score_step, t * SCORE_STEPS)
                step(dve.tensor_copy(so[:, :], held(t, slots)))
                dve.wait_ge(l1_q, t + 1)
                dve.wait_ge(l1_k_sb, t + 1)
                step(dve.tensor_tensor(prod, ps[:, 5, :], k_sb, ALU.mult))
                step(dve.tensor_reduce(s8[:, :], prod.rearrange("p (h d) -> p h d", h=HEADS), AX.X, ALU.add))
                dve.tensor_scalar(held(t, scores), s8[:, :], 1.0 / float(DK) ** 0.5, so[:, USED:USED + 1],
                                  ALU.mult, ALU.mult).then_inc(l1_tile, 1)
                assert step.n == SCORE_STEPS, step.n
                dve.wait_ge(l1_tile, t + 2)

            with dve.Fori(0, tiles) as t:
                step = Steps(dve, l2_step, t * LOOP2_STEPS)
                dve.tensor_copy(so[:, :], held(t, slots)).then_inc(l2_step, 1)
                dve.tensor_copy(s8[:, :], held(t, scores)).then_inc(l2_step, 1)
                dve.memset(m8[:, :], DIAG).then_inc(l2_step, 1)
                dve.memset(earlier[:, :], 0.0).then_inc(l2_step, 1)
                step.n = 4
                step(dve.tensor_copy(ahead[:, :], slot_id[:, bass.ds(t, 1)]))
                dve.sem_inc(v_passed, 1)
                with dve.Fori(0, tiles) as o:
                    turn = t * tiles + o
                    one = Steps(dve, row_step, turn * ROW_STEPS)
                    dve.tensor_copy(s_other[:, :], held(o, scores)).then_inc(row_step, 1)
                    one.n += 1
                    one(dve.tensor_copy(other[:, :], held(o, slots)[:, SUB1:KEY + 1]))
                    dve.tensor_tensor(diag[:, 8:10, :], eyes(2), spread(other[:, :], 2), ALU.mult).then_inc(id_diag, 1)
                    dve.tensor_tensor(diag[:, 0:HEADS, :], eyes(HEADS), spread(s_other[:, :], HEADS), ALU.mult).then_inc(s_diag, 1)
                    dve.wait_ge(id_row, turn + 1)
                    dve.tensor_scalar(same_row[:, :], ps[:, 7, 0:P], so[:, SUB1:SUB1 + 1], None, ALU.is_equal).then_inc(row_step, 1)
                    one.n += 1
                    one(dve.tensor_scalar(same_key[:, :], ps[:, 7, P:2 * P], so[:, KEY:KEY + 1], None, ALU.is_equal))
                    dve.tensor_scalar(same[:, :], same_row[:, :], -1.0, FAR, ALU.add, ALU.mult).then_inc(row_step, 1)
                    dve.wait_ge(row_step, one.base + one.n)
                    one.n += 1
                    dve.scalar_tensor_tensor(same_row[:, :], slot_col[:, :], ahead[:, :], same_row[:, :], ALU.is_lt, ALU.mult,
                                             accum_out=earlier[:, 2:3]).then_inc(row_step, 1)
                    one.n += 1
                    one(dve.scalar_tensor_tensor(same_key[:, :], slot_col[:, :], ahead[:, :], same_key[:, :], ALU.is_lt, ALU.mult,
                                                 accum_out=earlier[:, 3:4]))
                    dve.tensor_tensor(earlier[:, 0:2], earlier[:, 0:2], earlier[:, 2:4], ALU.add).then_inc(row_step, 1)
                    one.n += 1
                    one(dve.tensor_scalar(ahead[:, :], ahead[:, :], -float(P), None, ALU.add))
                    dve.wait_ge(s_row, turn + 1)
                    one(dve.tensor_tensor(far, ps[:, 5:7, :].rearrange("p b (h s) -> p (b h) s", s=P),
                                          same[:, :].rearrange("p (o s) -> p o s", o=1).to_broadcast([P, HEADS, P]), ALU.add))
                    one(dve.tensor_reduce(m_new[:, :], far, AX.X, ALU.max))
                    one(dve.tensor_tensor(m8[:, :], m8[:, :], m_new[:, :], ALU.max))
                    assert one.n == ROW_STEPS, one.n
                dve.tensor_tensor(ex[:, EX_S:EX_S + HEADS], s8[:, :], m8[:, :], ALU.subtract).then_inc(l2_step, 1)
                dve.tensor_scalar(ex[:, EX_0:EX_0 + HEADS], m8[:, :], -1.0, None, ALU.mult).then_inc(l2_step, 1)
                step.n += 2
                step(dve.tensor_scalar(ex[:, EX_D:EX_D + HEADS], m8[:, :], -1.0, DIAG, ALU.mult, ALU.add))
                dve.sem_inc(l2_arg, 1)
                step(dve.tensor_scalar(ex[:, EX_ONE:EX_ONE + 1], earlier[:, 1:2], 0.0, so[:, USED:USED + 1], ALU.is_equal, ALU.mult))
                step(dve.tensor_scalar(ex[:, EX_FIRST:EX_FIRST + 1], earlier[:, 0:1], 0.0, so[:, USED:USED + 1], ALU.is_equal, ALU.mult))
                dve.wait_ge(l2_exp, t + 1)
                step(dve.tensor_scalar(ex[:, EX_S:EX_S + HEADS], ex[:, EX_S:EX_S + HEADS], ex[:, EX_ONE:EX_ONE + 1], None, ALU.mult))
                step(dve.tensor_copy(held(t, exps), ex[:, :]))
                assert step.n == LOOP2_STEPS, step.n

            with dve.Fori(0, tiles) as t:
                step = Steps(dve, l3_step, t * LOOP3_STEPS)
                step(dve.tensor_copy(so[:, :], held(t, slots)))
                dve.tensor_scalar(diag[:, 8, :], ident[:, :], so[:, SUB1:SUB1 + 1], None, ALU.mult).then_inc(l3_diag, 1)
                dve.memset(z_sum[:, :], 0.0).then_inc(l3_step, 1)
                step.n += 1
                step(dve.tensor_copy(ex[:, :], held(t, exps)))
                dve.wait_ge(l3_row, t + 1)
                dve.sem_inc(v_passed, 1)
                with dve.Fori(0, tiles) as o:
                    turn = t * tiles + o
                    one = Steps(dve, sum_step, turn * SUM_STEPS)
                    dve.tensor_copy(ex_other[:, :], held(o, exps)).then_inc(sum_step, 1)
                    one.n += 1
                    one(dve.tensor_copy(other[:, 0:1], held(o, slots)[:, SUB1:SUB1 + 1]))
                    dve.tensor_scalar(same[:, :], ps[:, 7, 0:P], other[:, 0:1], None, ALU.is_equal).then_inc(l3_same, 1)
                    dve.wait_ge(l3_sum, turn + 1)
                    one(dve.tensor_tensor(z_sum[:, :], z_sum[:, :], ps[:, 6, 0:EX_N], ALU.add))
                    assert one.n == SUM_STEPS, one.n
                dve.wait_ge(l3_u, 16 * t + 16)
                step(dve.tensor_scalar(coef[:, 0:1], gath_u[:, H:H + 1], z_sum[:, EX_ONE:EX_ONE + 1], None, ALU.subtract))
                step(dve.scalar_tensor_tensor(zz[:, :], ex[:, EX_0:EX_0 + HEADS], coef[:, 0:1], ex[:, EX_D:EX_D + HEADS], ALU.mult, ALU.add))
                step(dve.tensor_tensor(zz[:, :], zz[:, :], z_sum[:, EX_S:EX_S + HEADS], ALU.add))
                step(dve.reciprocal(zz[:, :], zz[:, :]))
                step(dve.tensor_tensor(shares[:, :, :], ex[:, 0:3 * HEADS].rearrange("p (a h) -> p a h", a=3),
                                       zz[:, :].rearrange("p (o h) -> p o h", o=1).to_broadcast([P, 3, HEADS]), ALU.mult))
                step(dve.tensor_reduce(wcd[:, :], shares[:, :, :], AX.X, ALU.add))
                step(dve.tensor_scalar(wcd[:, :], wcd[:, :], 1.0 / HEADS, None, ALU.mult))
                dve.scalar_tensor_tensor(coef[:, 1:2], wcd[:, 1:2], ex[:, EX_ONE:EX_ONE + 1], wcd[:, 0:1], ALU.mult, ALU.subtract).then_inc(l3_step, 1)
                dve.tensor_tensor(coef[:, 2:3], wcd[:, 1:2], ex[:, EX_FIRST:EX_FIRST + 1], ALU.mult).then_inc(l3_step, 1)
                dve.tensor_tensor(held(t, change), gath_u[:, H + 2:H + 3], ex[:, EX_FIRST:EX_FIRST + 1], ALU.mult).then_inc(l3_step, 1)
                step.n += 3
                step(dve.tensor_scalar(coef[:, 3:4], wcd[:, 2:3], 1.0, ex[:, EX_FIRST:EX_FIRST + 1], ALU.add, ALU.mult))
                step(dve.scalar_tensor_tensor(coef[:, 3:4], coef[:, 2:3], gath_u[:, H + 1:H + 2], coef[:, 3:4], ALU.mult, ALU.subtract))
                dve.wait_ge(prod_free, t + 1)
                dve.wait_ge(l3_obj, 16 * t + 16)
                step(dve.tensor_scalar(prod, gath[:, 1, :], coef[:, 1:2], None, ALU.mult))
                step(dve.scalar_tensor_tensor(prod, gath_u[:, 0:H], coef[:, 2:3], prod, ALU.mult, ALU.subtract))
                dve.wait_ge(l3_sub, 16 * t + 16)
                dve.scalar_tensor_tensor(prod, gath[:, 0, :], coef[:, 3:4], prod, ALU.mult, ALU.subtract).then_inc(l3_tile, 1)
                assert step.n == LOOP3_STEPS, step.n

            with dve.Fori(0, tiles) as t:
                with dve.If(t > 0):
                    dve.wait_ge(bx_out, C)
                    for c in range(C):
                        dve.wait_ge(l4_done, C * t + c + 1)
                        dve.tensor_tensor(u[:, c, 0:H], u[:, c, 0:H], ps[:, 6 + c % 2, :], ALU.add).then_inc(l4_added, 1)
                    dve.wait_ge(l4_added, C * t + C)
                    dve.sem_inc(v_passed, 1)
                dve.sem_inc(l4_tile, 1)
                step = Steps(dve, l4_step, t * LOOP4_STEPS)
                step(dve.tensor_copy(so[:, :], held(t, slots)))
                dve.tensor_scalar(diag[:, 8, :], ident[:, :], so[:, SUB1:SUB1 + 1], None, ALU.mult).then_inc(l4_diag, 1)
                dve.wait_ge(row_free, t + 1)
                dve.memset(row_x, 0.0).then_inc(l4_step, 1)
                dve.tensor_copy(ex[:, EX_FIRST:EX_FIRST + 1], held(t, exps)[:, EX_FIRST:EX_FIRST + 1]).then_inc(l4_step, 1)
                dve.tensor_copy(coef[:, 0:1], held(t, change)).then_inc(l4_step, 1)
                step.n += 3
                step(dve.tensor_scalar(spot[:, 0:1], slot_id[:, 0:1], float(N), None, ALU.add))
                step(dve.tensor_tensor(spot[:, 1:2], so[:, SUB:SUB + 1], spot[:, 0:1], ALU.subtract))
                step(dve.scalar_tensor_tensor(spot[:, 2:3], spot[:, 1:2], ex[:, EX_FIRST:EX_FIRST + 1], spot[:, 0:1], ALU.mult, ALU.add))
                step(dve.tensor_copy(spot_i[:, :], spot[:, 2:3]))
                dve.wait_ge(nodes_ready, 1)
                step(dve.tensor_scalar(bm_e[:, :], node_row, so[:, SUB:SUB + 1], 2.0, ALU.is_equal, ALU.mult))
                dve.wait_ge(l4_bm, t * 32 + 32)
                step(dve.tensor_tensor(pair_rows[:, 0, :], pair_rows[:, 0, :], pair_rows[:, 1, :], ALU.add))
                step(dve.tensor_tensor(bm_e[:, 0:N], bm_e[:, 0:N], pair_rows[:, 0, :], ALU.add))
                dve.wait_ge(l4_row, t + 1)
                dve.sem_inc(v_passed, 1)
                with dve.Fori(0, tiles) as o:
                    turn = t * tiles + o
                    one = Steps(dve, total_step, turn * TOTAL_STEPS)
                    one(dve.tensor_copy(other[:, 0:1], held(o, slots)[:, SUB1:SUB1 + 1]))
                    dve.tensor_scalar(same[:, :], ps[:, 7, 0:P], other[:, 0:1], None, ALU.is_equal).then_inc(l4_same, 1)
                    dve.wait_ge(l4_sum, turn + 1)
                    one(dve.tensor_tensor(row_x, row_x, ps[:, 6, :], ALU.subtract))
                    assert one.n == TOTAL_STEPS, one.n
                dve.sem_inc(v_passed, 1)
                step(dve.bn_stats(stats[:, 0, :], row_x))
                dve.sem_inc(v_passed, 1)
                step(dve.bn_aggr(coef[:, 2:4], stats[:, 0, :]))
                dve.sem_inc(l4_var, 1)
                dve.wait_ge(l4_root, t + 1)
                step(dve.reciprocal(coef[:, 1:2], coef[:, 4:5]))
                step(dve.tensor_scalar(row_x, row_x, coef[:, 2:3], coef[:, 1:2], ALU.subtract, ALU.mult))
                dve.sem_inc(l4_x1, 1)
                dve.wait_ge(l4_x0, t * 16 + 16)
                step(dve.tensor_tensor(row_x0, row_x, row_x0, ALU.subtract))
                step(dve.tensor_scalar(dz[:, 0, :], row_x0, coef[:, 0:1], None, ALU.mult))
                step(dve.scalar_tensor_tensor(dz[:, 1, :], row_x0, coef[:, 0:1], dz[:, 0, :], ALU.mult, ALU.subtract))
                dve.sem_inc(l4_dz, 1)
                assert step.n == LOOP4_STEPS, step.n

            for i in range(C + 1):
                if i < C:
                    dve.wait_ge(last_done, i + 1)
                    if i == 0:
                        dve.wait_ge(bx_out, C)
                    dve.tensor_tensor(u[:, i, 0:H], u[:, i, 0:H], ps[:, 6 + i % 2, :], ALU.add).then_inc(last_added, 1)
                if i:
                    dve.wait_ge(zt_hi, i)
                    dve.scalar_tensor_tensor(terms[:, 1, i - 1, :], u[:, i - 1, 0:H], dinv_z[:, i - 1:i], terms[:, 0, i - 1, :],
                                             ALU.mult, ALU.subtract).then_inc(zt_lo, 1)
            dve.wait_ge(x1_in, 16 * C)
            for i in range(C):
                dve.wait_ge(y_done, i + 1)
                dve.scalar_tensor_tensor(xs[:, i, :], ps[:, i % 8, :], 1.0 / ZS, xs[:, i, :],
                                         ALU.mult, ALU.add).then_inc(y_added, 1)
                dve.wait_ge(y_added, i + 1)
                main(dve.bn_stats(stats[:, i, :], xs[:, i, :]))
                dve.bn_aggr(mv[:, i, :], stats[:, i, :]).then_inc(var1, 1)
                dve.wait_ge(std1, i + 1)
                main(dve.reciprocal(rstd[:, i:i + 1], std[:, i:i + 1]))
                dve.tensor_scalar(xs[:, i, :], xs[:, i, :], mv[:, i, 0:1], rstd[:, i:i + 1],
                                  ALU.subtract, ALU.mult).then_inc(scaled, 1)


def kernel(x, adj, L0_gnn_rel_pair_index, L0_gnn_Wq, L0_gnn_bq, L0_gnn_Wk, L0_gnn_bk):
    import numpy as np
    import concourse.bacc as bacc
    from concourse.bass_utils import run_bass_kernel_spmd

    laid_out = {
        "x": np.ascontiguousarray(x),
        "adj": np.ascontiguousarray(adj),
        "adj_t": np.ascontiguousarray(np.asarray(adj).T),
        "pairs": np.ascontiguousarray(L0_gnn_rel_pair_index),
        "wq_t": np.ascontiguousarray(np.asarray(L0_gnn_Wq).T),
        "bq": np.ascontiguousarray(L0_gnn_bq),
        "wk_t": np.ascontiguousarray(np.asarray(L0_gnn_Wk).T),
        "bk": np.ascontiguousarray(L0_gnn_bk),
    }
    nc = bacc.Bacc("TRN2", target_bir_lowering=False, num_devices=1)
    args = [nc.dram_tensor(f"in_{k}", a.shape, mybir.dt.from_np(a.dtype), kind="ExternalInput").ap() for k, a in laid_out.items()]
    out = nc.dram_tensor("out", (N, H), f32, kind="ExternalOutput").ap()
    build(nc, *args, out)
    r = run_bass_kernel_spmd(nc, [{f"in_{k}": a for k, a in laid_out.items()}], core_ids=[0])
    return r.results[0]["out"]
```
